# Optimizing a Trainium2 kernel written in Bass

```python
import numpy as np
import jax
import jax.numpy as jnp

def _softmax(x, axis=-1):
    return jax.nn.softmax(x, axis=axis)

def _gelu(x):
    return jax.nn.gelu(x, approximate=True)

def _silu(x):
    return jax.nn.silu(x)

def _sigmoid(x):
    return jax.nn.sigmoid(x)

def _layernorm(x, axis=-1, eps=1e-05):
    m = jnp.mean(x, axis=axis, keepdims=True)
    v = jnp.var(x, axis=axis, keepdims=True)
    return (x - m) / jnp.sqrt(v + eps)

def _scatter_add(tgt, idx, src, axis=0):
    return tgt.at[idx].add(src)

def _segment_sum(src, seg, n):
    return jax.ops.segment_sum(src, seg, n)
kernel_name = 'mk_decoder_postln_d1_seqx_r4_7480cc'

def setup_inputs(seed: int=0):
    np.random.seed(seed)
    _w = jnp.asarray

    def _rec_inputs():
        import jax
        import jax.numpy as jnp
        _rk = jax.random.key(seed)
        x = 7.22e-05 + 1 * jax.random.normal(jax.random.fold_in(_rk, 1), (16, 112, 512), jnp.float32)
        _lenS = 112 - jax.random.randint(jax.random.fold_in(_rk, 7), (16,), 0, max(1, 112 // 4) + 1, jnp.int32)
        _lenS2 = 375 - jax.random.randint(jax.random.fold_in(_rk, 8), (16,), 0, max(1, 375 // 4) + 1, jnp.int32)
        _ctx_2048P = jax.random.normal(jax.random.fold_in(_rk, 11), (16, 16, 512), jnp.float32)
        _ctx_2048c = jax.random.dirichlet(jax.random.fold_in(_rk, 511), 0.3 * jnp.ones((16,), jnp.float32), (16, 375))
        _ctx_2048t = jnp.einsum('bsk,bkd->bsd', _ctx_2048c, _ctx_2048P)
        _ctx_2048t = _ctx_2048t * jax.lax.rsqrt(jnp.mean(jnp.square(_ctx_2048t)) + 1e-12) * 0.953939
        ctx_2048 = -0.000514642 + 1.00011 * (_ctx_2048t + 0.3 * jax.random.normal(jax.random.fold_in(_rk, 611), (16, 375, 512), jnp.float32))
        return (x, ctx_2048)
    x, ctx_2048 = _rec_inputs()

    def _L0_attn_setup():
        import jax, jax.numpy as jnp
        import numpy as np
        import math
        D = 512
        K = 64
        NUM_HEADS = 32
        HEAD_DIM = K // NUM_HEADS
        SPARSITY = 0.1
        LN_EPS = 1e-05
        key = jax.random.key(seed)
        ks = jax.random.split(key, 12)
        B, S = (1, 256)
        sc = 0.02
        inp = {'x': jax.random.normal(ks[0], (B, S, D), dtype=jnp.float32), 'gamma': jnp.ones((D,), jnp.float32), 'beta': jnp.zeros((D,), jnp.float32), 'W1': jax.random.normal(ks[1], (128, D), jnp.float32) * sc, 'b1': jnp.zeros((128,), jnp.float32), 'W2': jax.random.normal(ks[2], (64, 128), jnp.float32) * sc, 'b2': jnp.zeros((64,), jnp.float32), 'W3': jax.random.normal(ks[3], (1, 64), jnp.float32) * sc, 'b3': jnp.zeros((1,), jnp.float32), 'Wqkv': jax.random.normal(ks[4], (3 * K, D), jnp.float32) * sc, 'bqkv': jnp.zeros((3 * K,), jnp.float32), 'Wout': jax.random.normal(ks[5], (D, K), jnp.float32) * sc, 'bout': jnp.zeros((D,), jnp.float32)}
        return inp
    _L0_attn_all = _L0_attn_setup()
    _L0_attn_in = {k: v for k, v in _L0_attn_all.items() if k in ('gamma', 'beta', 'W1', 'b1', 'W2', 'b2', 'W3', 'b3', 'Wqkv', 'bqkv', 'Wout', 'bout')}
    del _L0_attn_all

    def _L0_xattn_setup():
        import jax, jax.numpy as jnp
        import numpy as np
        D_MODEL = 512
        NUM_HEADS = 16
        HEAD_DIM = D_MODEL // NUM_HEADS

        def _fq_sym(x, axis):
            s = jnp.max(jnp.abs(x), axis=axis, keepdims=True) / 127.0
            s = jnp.maximum(s, 1e-08)
            q = jnp.clip(jnp.round(x / s), -127.0, 127.0) * s
            return x + jax.lax.stop_gradient(q - x)

        def _fq_unsigned(x, axis):
            s = jnp.max(x, axis=axis, keepdims=True) / 255.0
            s = jnp.maximum(s, 1e-08)
            q = jnp.clip(jnp.round(x / s), 0.0, 255.0) * s
            return x + jax.lax.stop_gradient(q - x)
        key = jax.random.key(seed)
        ks = jax.random.split(key, 8)
        B, N, M, C = (2, 512, 128, D_MODEL)
        return {'x': jax.random.normal(ks[0], (B, N, C), jnp.float32), 'cond': jax.random.normal(ks[1], (B, M, C), jnp.float32), 'Wq': jax.random.normal(ks[2], (C, C), jnp.float32) * 0.02, 'bq': jnp.zeros((C,), jnp.float32), 'Wkv': jax.random.normal(ks[3], (C, 2 * C), jnp.float32) * 0.02, 'bkv': jnp.zeros((2 * C,), jnp.float32), 'Wp': jax.random.normal(ks[4], (C, C), jnp.float32) * 0.02, 'bp': jnp.zeros((C,), jnp.float32)}
    _L0_xattn_all = _L0_xattn_setup()
    _L0_xattn_in = {k: v for k, v in _L0_xattn_all.items() if k in ('Wq', 'bq', 'Wkv', 'bkv', 'Wp', 'bp')}
    del _L0_xattn_all

    def _L0_ffn_setup():
        import jax, jax.numpy as jnp
        import numpy as np
        EPS = 1e-08

        def _quantize(w):
            gamma = jnp.mean(jnp.abs(w))
            return jnp.clip(jnp.round(w / (gamma + EPS)), -1.0, 1.0)

        def _bitlinear(x, w):
            return jnp.matmul(x, _quantize(w).T)
        key = jax.random.key(seed)
        k1, k2, k3, k4 = jax.random.split(key, 4)
        d, h = (512, 1408)
        x = jax.random.normal(k1, (4, 512, d), dtype=jnp.float32)
        w1 = jax.random.normal(k2, (h, d), dtype=jnp.float32)
        w2 = jax.random.normal(k3, (h, d), dtype=jnp.float32)
        w3 = jax.random.normal(k4, (d, h), dtype=jnp.float32)
        return {'x': x, 'w1': w1, 'w2': w2, 'w3': w3}
    _L0_ffn_all = _L0_ffn_setup()
    _L0_ffn_in = {k: v for k, v in _L0_ffn_all.items() if k in ('w1', 'w2', 'w3')}
    del _L0_ffn_all
    return {'x': x, 'ctx_2048': ctx_2048, 'L0_attn_gamma': _L0_attn_in['gamma'], 'L0_attn_beta': _L0_attn_in['beta'], 'L0_attn_W1': _L0_attn_in['W1'], 'L0_attn_b1': _L0_attn_in['b1'], 'L0_attn_W2': _L0_attn_in['W2'], 'L0_attn_b2': _L0_attn_in['b2'], 'L0_attn_W3': _L0_attn_in['W3'], 'L0_attn_b3': _L0_attn_in['b3'], 'L0_attn_Wqkv': _L0_attn_in['Wqkv'], 'L0_attn_bqkv': _L0_attn_in['bqkv'], 'L0_attn_Wout': _L0_attn_in['Wout'], 'L0_attn_bout': _L0_attn_in['bout'], 'L0_xattn_Wq': _L0_xattn_in['Wq'], 'L0_xattn_bq': _L0_xattn_in['bq'], 'L0_xattn_Wkv': _L0_xattn_in['Wkv'], 'L0_xattn_bkv': _L0_xattn_in['bkv'], 'L0_xattn_Wp': _L0_xattn_in['Wp'], 'L0_xattn_bp': _L0_xattn_in['bp'], 'L0_ffn_w1': _L0_ffn_in['w1'], 'L0_ffn_w2': _L0_ffn_in['w2'], 'L0_ffn_w3': _L0_ffn_in['w3']}

def reference(x, ctx_2048, L0_attn_gamma, L0_attn_beta, L0_attn_W1, L0_attn_b1, L0_attn_W2, L0_attn_b2, L0_attn_W3, L0_attn_b3, L0_attn_Wqkv, L0_attn_bqkv, L0_attn_Wout, L0_attn_bout, L0_xattn_Wq, L0_xattn_bq, L0_xattn_Wkv, L0_xattn_bkv, L0_xattn_Wp, L0_xattn_bp, L0_ffn_w1, L0_ffn_w2, L0_ffn_w3):
    import jax
    import jax.numpy as jnp

    def _L0_attn_ref(x, gamma, beta, W1, b1, W2, b2, W3, b3, Wqkv, bqkv, Wout, bout):
        import jax, jax.numpy as jnp
        import numpy as np
        import math
        D = 512
        K = 64
        NUM_HEADS = 32
        HEAD_DIM = K // NUM_HEADS
        SPARSITY = 0.1
        LN_EPS = 1e-05
        B, S, d = x.shape
        mu = jnp.mean(x, -1, keepdims=True)
        var = jnp.var(x, -1, keepdims=True)
        xn = (x - mu) * jax.lax.rsqrt(var + LN_EPS) * gamma + beta
        h = jnp.einsum('bsd,fd->bsf', xn, W1)
        pair = jax.nn.relu(h[:, :, None, :] - h[:, None, :, :] + b1)
        pair = jax.nn.relu(jnp.einsum('bijf,gf->bijg', pair, W2) + b2)
        sim = jnp.einsum('bijg,og->bijo', pair, W3)[..., 0] + b3[0]
        diag = jnp.arange(S)
        sim = sim.at[:, diag, diag].set(0.0)
        k_sparse = max(1, int(S * SPARSITY))
        _, top_idx = jax.lax.top_k(sim, k_sparse)
        mask = jnp.full((B, S, S), -jnp.inf, dtype=x.dtype)
        bidx = jnp.arange(B)[:, None, None]
        iidx = jnp.arange(S)[None, :, None]
        mask = mask.at[bidx, iidx, top_idx].set(0.0)
        qkv = jnp.einsum('bsd,ed->bse', xn, Wqkv) + bqkv
        q, k, v = jnp.split(qkv, 3, axis=-1)

        def heads(t):
            return t.reshape(B, S, NUM_HEADS, HEAD_DIM).transpose(0, 2, 1, 3)
        q, k, v = (heads(q), heads(k), heads(v))
        scores = jnp.einsum('bhid,bhjd->bhij', q, k) / math.sqrt(HEAD_DIM)
        scores = scores + mask[:, None, :, :]
        attn = jax.nn.softmax(scores, axis=-1)
        ao = jnp.einsum('bhij,bhjd->bhid', attn, v)
        ao = ao.transpose(0, 2, 1, 3).reshape(B, S, K)
        out = jnp.einsum('bsk,dk->bsd', ao, Wout) + bout
        return x + out

    def _L0_xattn_ref(x, cond, Wq, bq, Wkv, bkv, Wp, bp):
        import jax, jax.numpy as jnp
        import numpy as np
        D_MODEL = 512
        NUM_HEADS = 16
        HEAD_DIM = D_MODEL // NUM_HEADS

        def _fq_sym(x, axis):
            s = jnp.max(jnp.abs(x), axis=axis, keepdims=True) / 127.0
            s = jnp.maximum(s, 1e-08)
            q = jnp.clip(jnp.round(x / s), -127.0, 127.0) * s
            return x + jax.lax.stop_gradient(q - x)

        def _fq_unsigned(x, axis):
            s = jnp.max(x, axis=axis, keepdims=True) / 255.0
            s = jnp.maximum(s, 1e-08)
            q = jnp.clip(jnp.round(x / s), 0.0, 255.0) * s
            return x + jax.lax.stop_gradient(q - x)
        B, N, C = x.shape
        H, hd = (NUM_HEADS, HEAD_DIM)
        q = (x @ Wq + bq).reshape(1, B * N, H, hd)
        kv = (cond @ Wkv + bkv).reshape(1, -1, 2, H, hd)
        k, v = (kv[:, :, 0], kv[:, :, 1])
        scale = 1.0 / np.sqrt(hd).astype(np.float32)
        q = jnp.transpose(q * scale, (0, 2, 1, 3))
        k = jnp.transpose(k, (0, 2, 1, 3))
        v = jnp.transpose(v, (0, 2, 1, 3))
        q = _fq_sym(q, axis=-1)
        k = _fq_sym(k, axis=-1)
        v = _fq_sym(v, axis=2)
        attn = jnp.einsum('bhqd,bhkd->bhqk', q, k)
        attn = jax.nn.softmax(attn.astype(jnp.float32), axis=-1)
        attn = _fq_unsigned(attn, axis=-1)
        out = jnp.einsum('bhqk,bhkd->bhqd', attn, v)
        out = jnp.transpose(out, (0, 2, 1, 3)).reshape(B, N, C)
        return out @ Wp + bp

    def _L0_ffn_ref(x, w1, w2, w3):
        import jax, jax.numpy as jnp
        import numpy as np
        EPS = 1e-08

        def _quantize(w):
            gamma = jnp.mean(jnp.abs(w))
            return jnp.clip(jnp.round(w / (gamma + EPS)), -1.0, 1.0)

        def _bitlinear(x, w):
            return jnp.matmul(x, _quantize(w).T)
        x1 = _bitlinear(x, w1)
        x2 = _bitlinear(x, w2)
        hidden = jax.nn.sigmoid(x1) * x2
        return _bitlinear(hidden, w3)
    x = _layernorm(x + _L0_attn_ref(x, L0_attn_gamma, L0_attn_beta, L0_attn_W1, L0_attn_b1, L0_attn_W2, L0_attn_b2, L0_attn_W3, L0_attn_b3, L0_attn_Wqkv, L0_attn_bqkv, L0_attn_Wout, L0_attn_bout), axis=-1)
    x = _layernorm(x + _L0_xattn_ref(x, ctx_2048, L0_xattn_Wq, L0_xattn_bq, L0_xattn_Wkv, L0_xattn_bkv, L0_xattn_Wp, L0_xattn_bp), axis=-1)
    x = _layernorm(x + _L0_ffn_ref(x, L0_ffn_w1, L0_ffn_w2, L0_ffn_w3), axis=-1)
    return x

_drawn_inputs = setup_inputs


def setup_inputs(seed=0):
    import zlib

    import numpy as np

    out = dict(_drawn_inputs(seed))
    spreads = {'L0_attn_gamma': (1.0, 0.6),
     'L0_attn_beta': (0.0, 0.8),
     'L0_attn_b1': (0.0, 2.0),
     'L0_attn_b2': (0.0, 2.0),
     'L0_attn_bqkv': (0.0, 0.606),
     'L0_attn_bout': (0.0, 0.1),
     'L0_xattn_bq': (0.0, 0.8),
     'L0_xattn_bkv': (0.0, 0.1),
     'L0_xattn_bp': (0.0, 0.1)}
    factors = {'L0_attn_W1': 2.833, 'L0_attn_W2': 2.793, 'L0_attn_W3': 2.71, 'L0_xattn_Wq': 8.0}
    for name, (base, spread) in spreads.items():
        noise = np.random.default_rng([zlib.crc32(name.encode()), seed]).standard_normal(out[name].shape)
        drawn = base * np.exp(spread * noise) if base else spread * noise
        out[name] = jnp.asarray(drawn.astype(out[name].dtype))
    for name, factor in factors.items():
        out[name] = (out[name] * factor).astype(out[name].dtype)
    return out
```

```python
from contextlib import ExitStack

import numpy as np

import concourse.bass as bass
from concourse import mybir

ALU = mybir.AluOpType
ACT = mybir.ActivationFunctionType
F32 = mybir.dt.float32
BF16 = mybir.dt.bfloat16
FP16 = mybir.dt.float16
U16 = mybir.dt.uint16
X = mybir.AxisListType.X
ds = bass.ds

B, S, D = 16, 112, 512
ROWS = B * S
P = 128
RT = ROWS // P
DC = D // P
F1, F2 = 128, 64
SH, SD = 32, 2
SK = SH * SD
TOP = max(1, int(S * 0.1))
GI = 8
NG = S // GI
EPS = 1e-5
FLOOR = -3.0e38
CTX = 375
KEYS = B * CTX
H, HD = 16, 32
KT = 125
NKT = KEYS // KT
NEXP = 3
MAGIC = 1.5 * 2.0 ** 23
FFN = 1408
MC = FFN // P


class Chain:

    def __init__(self, eng, sem, base=0):
        self.eng, self.sem, self.base, self.n = eng, sem, base, 0

    def link(self, ins, carrier=None):
        self.n += 1
        ins.then_inc(self.sem, 1)
        self.eng.wait_ge(self.sem, self.base + self.n)
        if carrier is not None:
            self.eng.memset(carrier, 0.0)


def rstd_newton(dve, chain, rstd, var, tmp):
    chain.link(dve.tensor_tensor(tmp, var, rstd, ALU.mult))
    chain.link(dve.tensor_tensor(tmp, tmp, rstd, ALU.mult))
    chain.link(dve.tensor_scalar(tmp, tmp, -0.5, 1.5, ALU.mult, ALU.add))
    chain.link(dve.tensor_tensor(rstd, rstd, tmp, ALU.mult))


def sparse_attention(nc, a, aoT):
    POSTL = 18
    PREPL = 5
    with ExitStack() as ctx:
        def sb(name, shape, dt=F32):
            return ctx.enter_context(nc.sbuf_tensor("p1_" + name, shape, dt))

        def pb(name, shape, dt=F32):
            return ctx.enter_context(nc.psum_tensor("p1_" + name, shape, dt))

        def sem(name):
            return ctx.enter_context(nc.semaphore("p1_" + name))

        xa = sb("xa", [S, B * D])
        w1 = sb("w1", [P, DC, F1])
        wqkv = sb("wqkv", [P, DC, 3 * SK])
        gamma, beta = sb("gamma", [P, DC]), sb("beta", [P, DC])
        b1, b2 = sb("b1", [P, 1]), sb("b2", [P, 1])
        w2 = sb("w2", [F1, F2])
        w3 = sb("w3", [P, 2])
        b3 = sb("b3", [S, 1])
        bqkv = sb("bqkv", [S, 3 * SK])
        ident = sb("ident", [P, P])
        identb = sb("identb", [S, S], BF16)
        tri = sb("tri", [S, S], BF16)
        offdiag = sb("offdiag", [S, S])
        rank = sb("rank", [S, TOP, S], BF16)

        stats = sb("stats", [S, B * 6])
        mv = sb("mv", [S, B, 2])
        var, mean, rstd, tmp = (sb(n, [S, B]) for n in ("var", "mean", "rstd", "tmp"))
        xn = sb("xn", [S, D])
        xnT = sb("xnT", [P, DC, S])
        hb = sb("hb", [F1, 2, S])
        hn = sb("hn", [F1, 2, S])
        qkv = sb("qkv", [S, 2, 3 * SK])
        kvp = sb("kvp", [S, 2, 3, 2 * SK], BF16)
        kvr = sb("kvr", [S, 2, 2 * SK])
        pair = sb("pair", [F1, 2, GI * S])
        u = sb("u", [P, 2, GI // 2 * S])
        simT = sb("simT", [S, S])
        sim = sb("sim", [S, S])
        best = sb("best", [S, 16])
        wait_col = sb("wait_col", [S, 1])
        rest, rest2 = sb("rest", [S, S]), sb("rest2", [S, S])
        mask = sb("mask", [S, S], BF16)
        maskT = sb("maskT", [S, S], BF16)
        rankT = sb("rankT", [S, S], BF16)
        onehot = sb("onehot", [S, TOP, S], BF16)
        prod = sb("prod", [S, TOP, SK])
        sc, ex = sb("sc", [S, TOP, SH]), sb("ex", [S, TOP, SH])
        mx, den, rden = sb("mx", [S, SH]), sb("den", [S, SH]), sb("rden", [S, SH])
        ao = sb("ao", [S, P])

        ps_xT = pb("ps_xT", [P, DC, P])
        ps_hq = pb("ps_hq", [P, 512])
        ps_u = pb("ps_u", [P, 2, 512])
        ps_simT = pb("ps_simT", [S, 512])
        ps_one = pb("ps_one", [P, 512])
        ps_g = pb("ps_g", [S, 2, 512])
        NH1 = 512 // SK

        s_in = sem("s_in")
        s_w3z, s_aoz, s_stat, s_sqrt = sem("s_w3z"), sem("s_aoz"), sem("s_stat"), sem("s_sqrt")
        s_pc, s_prep, s_start = sem("s_pc"), sem("s_prep"), sem("s_start")
        s_xn, s_xT, s_xnT, s_hq, s_hb, s_hn, s_kvp = (sem(n) for n in ("s_xn", "s_xT", "s_xnT", "s_hq", "s_hb", "s_hn", "s_kvp"))
        s_pairv, s_paira, s_mm1, s_u, s_mm2 = (sem(n) for n in ("s_pairv", "s_paira", "s_mm1", "s_u", "s_mm2"))
        s_simT, s_sim, s_mask, s_mT, s_mTs, s_cum, s_oh = (sem(n) for n in ("s_simT", "s_sim", "s_mask", "s_mT", "s_mTs", "s_cum", "s_oh"))
        s_gk, s_sc, s_ex, s_gv, s_ao, s_aoT, s_aoTs = (sem(n) for n in ("s_gk", "s_sc", "s_ex", "s_gv", "s_ao", "s_aoT", "s_aoTs"))

        DV = 7
        loads = [
            (xa[:].rearrange("s (b d) -> s b d", b=B), a["x"].rearrange("b s d -> s b d")),
            (w1[:], a["W1T"].rearrange("(c p) f -> p c f", p=P)),
            (wqkv[:], a["WqkvT"].rearrange("(c p) f -> p c f", p=P)),
            (gamma[:], a["gamma"]),
            (beta[:], a["beta"]),
            (b1[:], a["b1"].rearrange("(p a) -> p a", a=1)),
            (b2[0:F2], a["b2"].rearrange("(p a) -> p a", a=1)),
            (b2[F2:P], a["b2"].rearrange("(p a) -> p a", a=1)),
            (w2[:], a["W2T"]),
            (b3[:], a["b3"].rearrange("(p a) -> p a", a=1).broadcast_to([S, 1])),
            (bqkv[:], a["bqkv"].rearrange("(p a) -> p a", p=1).broadcast_to([S, 3 * SK])),
            (ident[:], a["ident"]), (identb[:], a["identb"][0:S, 0:S]), (tri[:], a["tri"]),
            (offdiag[:], a["offdiag"]), (rank[:], a["rank"]),
        ]
        LOADED = 16 * len(loads) + 32

        def schedule(eng_steps, pair_step, last=None):
            for g in range(NG):
                pair_step(g)
                for step in eng_steps.get(g, ()):
                    step()
            if last:
                last()

        def batches(eng, run):
            run(0, 0, post=False, prep=True)
            with eng.Fori(0, (B - 2) // 2) as k:
                for half in range(2):
                    run(2 * k + 1 + half, (1 + half) % 2, post=True, prep=True)
            run(B - 1, (B - 1) % 2, post=True, prep=False)
            run(B, 0, post=True, prep=False)

        block = ctx.enter_context(nc.Block())

        @block.sync
        def _(sp):
            for out, src in loads:
                sp.dma_start(out, src).then_inc(s_in, 16)
            sp.wait_ge(s_w3z, 1)
            w3col = a["W3"].rearrange("a f -> f a")
            sp.dma_start(w3[0:F2, 0:1], w3col).then_inc(s_in, 16)
            sp.dma_start(w3[F2:P, 1:2], w3col).then_inc(s_in, 16)

        @block.vector
        def _(dve):
            dve.memset(w3[:], 0.0).then_inc(s_w3z, 1)
            dve.memset(ao[:], 0.0).then_inc(s_aoz, 1)
            dve.wait_ge(s_in, LOADED)
            dve.wait_ge(s_aoz, 1)
            start = Chain(dve, s_start)
            with dve.Fori(0, B) as b:
                dve.bn_stats(stats[:, ds(b * 6, 6)], xa[:, ds(b * D, D)]).then_inc(s_stat, 1)
            dve.wait_ge(s_stat, B)
            for b in range(B):
                dve.bn_aggr(mv[:, b, :], stats[:, 6 * b:6 * b + 6]).then_inc(s_stat, 1)
            dve.wait_ge(s_stat, 2 * B)
            start.link(dve.tensor_scalar(var[:], mv[:, :, 1], EPS, None, ALU.add))
            start.link(dve.tensor_copy(mean[:], mv[:, :, 0]))
            dve.wait_ge(s_sqrt, 1)
            start.link(dve.reciprocal(rstd[:], tmp[:]))
            rstd_newton(dve, start, rstd[:], var[:], tmp[:])

            def normalise(b):
                if not isinstance(b, int) or b > 0:
                    dve.wait_ge(s_xT, b)
                dve.tensor_scalar(xn[:], xa[:, ds(b * D, D)], mean[:, ds(b, 1)], rstd[:, ds(b, 1)],
                                  ALU.subtract, ALU.mult).then_inc(s_xn, 1)

            def project(b, par):
                dve.wait_ge(s_hb, b + 1)
                c = Chain(dve, s_prep, PREPL * b)
                dve.tensor_scalar(hn[:, par, :], ps_hq[:, 0:S], -1.0, None, ALU.mult).then_inc(s_hn, 1)
                c.link(dve.tensor_tensor(qkv[:, par, :], ps_hq[0:S, 256:256 + 3 * SK], bqkv[:], ALU.add))
                kv = qkv[:, par, SK:3 * SK]
                c.link(dve.tensor_copy(kvp[:, par, 0, :], kv))
                c.link(dve.tensor_tensor(kvr[:, 0, :], kv, kvp[:, par, 0, :], ALU.subtract))
                c.link(dve.tensor_copy(kvp[:, par, 1, :], kvr[:, 0, :]))
                c.link(dve.tensor_tensor(kvr[:, 1, :], kvr[:, 0, :], kvp[:, par, 1, :], ALU.subtract))
                dve.tensor_copy(kvp[:, par, 2, :], kvr[:, 1, :]).then_inc(s_kvp, 1)

            def topk(b, c):
                dve.wait_ge(s_sim, b + 1)
                c.link(dve.tensor_tensor(sim[:], ps_one[0:S, 0:S], offdiag[:], ALU.mult), wait_col[:])
                c.link(dve.max(best[:, 0:8], sim[:]), wait_col[:])
                c.link(dve.match_replace(rest[:], best[:, 0:8], sim[:], FLOOR), wait_col[:])
                c.link(dve.max(best[:, 8:16], rest[:]))
                c.link(dve.memset(best[:, TOP:16], FLOOR), wait_col[:])
                c.link(dve.match_replace(rest2[:], best[:, 8:16], rest[:], FLOOR))
                dve.tensor_scalar(mask[:], rest2[:], FLOOR, None, ALU.is_equal).then_inc(s_mask, 1)

            def onehots(b, c):
                dve.wait_ge(s_cum, b + 1)
                c.link(dve.tensor_tensor(rankT[:], ps_one[0:S, 0:S], maskT[:], ALU.mult))
                dve.tensor_tensor(onehot[:], rankT[:].unsqueeze(1).broadcast_to([S, TOP, S]), rank[:],
                                  ALU.is_equal).then_inc(s_oh, 1)

            def scores(b, par, c):
                dve.wait_ge(s_gk, b + 1)
                q = qkv[:, par, 0:SK].unsqueeze(1)
                for lo, hi in ((0, NH1), (NH1, TOP)):
                    c.link(dve.tensor_tensor(prod[:, lo:hi, :],
                                             ps_g[:, lo // NH1, 0:(hi - lo) * SK].rearrange("s (t e) -> s t e", e=SK),
                                             q.broadcast_to([S, hi - lo, SK]), ALU.mult))
                pr = prod[:].rearrange("s t (h e) -> s (t h) e", e=SD)
                c.link(dve.tensor_tensor(sc[:].rearrange("s t h -> s (t h)"), pr[:, :, 0], pr[:, :, 1], ALU.add))
                c.link(dve.tensor_reduce(mx[:], sc[:].rearrange("s t h -> s h t"), X, ALU.max))
                dve.tensor_tensor(sc[:], sc[:], mx[:].unsqueeze(1).broadcast_to([S, TOP, SH]),
                                  ALU.subtract).then_inc(s_sc, 1)

            def mix(b, c):
                dve.wait_ge(s_ex, b + 1)
                c.link(dve.tensor_reduce(den[:], ex[:].rearrange("s t h -> s h t"), X, ALU.add))
                c.link(dve.reciprocal(rden[:], den[:]))
                dve.wait_ge(s_gv, b + 1)
                for e in range(SD):
                    for lo, hi in ((0, NH1), (NH1, TOP)):
                        g = ps_g[:, lo // NH1, 0:(hi - lo) * SK].rearrange("s (t h e) -> s t h e", h=SH, e=SD)
                        o = prod[:].rearrange("s t (h e) -> s t h e", e=SD)
                        c.link(dve.tensor_tensor(o[:, lo:hi, :, e], g[:, :, :, e], ex[:, lo:hi, :], ALU.mult))
                c.link(dve.tensor_reduce(ao[:, 0:SK], prod[:].rearrange("s t k -> s k t"), X, ALU.add))
                dve.tensor_tensor(ao[:, 0:SK].rearrange("s (h e) -> s h e", e=SD), ao[:, 0:SK].rearrange("s (h e) -> s h e", e=SD),
                                  rden[:].unsqueeze(2).broadcast_to([S, SH, SD]), ALU.mult).then_inc(s_ao, 1)

            def run(b, par, post, prep):
                steps = {}
                if post:
                    c = Chain(dve, s_pc, (b - 1) * POSTL)
                    steps = {2: [lambda: topk(b - 1, c)], 4: [lambda: mask_copy(b - 1)],
                             6: [lambda: onehots(b - 1, c)], 8: [lambda: scores(b - 1, 1 - par, c)],
                             10: [lambda: mix(b - 1, c)]}
                if prep:
                    steps[0] = [lambda: normalise(b + 1)]
                    steps[12] = [lambda: project(b + 1, 1 - par)]
                if isinstance(b, int) and b == B:
                    for g in sorted(steps):
                        for step in steps[g]:
                            step()
                else:
                    def pairs(g):
                        if g == 0:
                            dve.wait_ge(s_hn, b + 1)
                            dve.wait_ge(s_hb, b + 1)
                        if g >= 2:
                            dve.wait_ge(s_mm1, NG * b + g - 1)
                        elif not isinstance(b, int) or b > 0:
                            dve.wait_ge(s_mm1, NG * b + g - 1)
                        for r in range(DV):
                            i = GI * g + r
                            ins = dve.tensor_scalar(pair[:, g % 2, r * S:(r + 1) * S], hn[:, par, :],
                                                    hb[:, par, i:i + 1], 0.0, ALU.add, ALU.max)
                        ins.then_inc(s_pairv, 1)
                    schedule(steps, pairs)
                if post:
                    assert c.n <= POSTL, c.n
                    used.append(c.n)

            def mask_copy(b):
                dve.wait_ge(s_mT, b + 1)
                dve.tensor_copy(maskT[:], ps_one[:].bitcast(BF16)[0:S, 0:S]).then_inc(s_mTs, 1)

            used = []
            normalise(0)
            project(0, 0)
            batches(dve, run)
            assert set(used) == {POSTL}, used

        @block.scalar
        def _(act):
            act.wait_ge(s_start, 2)
            act.activation(tmp[:], var[:], ACT.Sqrt).then_inc(s_sqrt, 1)
            act.preload_act_table(ACT.Exp)

            def evac_x(b):
                act.wait_ge(s_xT, b + 1)
                for c in range(DC):
                    act.activation(xnT[:, c, :], ps_xT[:, c, 0:S], ACT.Identity, bias=beta[:, c:c + 1],
                                   scale=gamma[:, c:c + 1]).then_inc(s_xnT, 1)

            def evac_h(b, par):
                act.wait_ge(s_hq, b + 1)
                act.activation(hb[:, par, :], ps_hq[:, 0:S], ACT.Identity, bias=b1[:, 0:1]).then_inc(s_hb, 1)

            def evac_sim(b):
                act.wait_ge(s_mm2, NG * (b + 1))
                act.activation(simT[:], ps_simT[:, 0:S], ACT.Identity, bias=b3[:, 0:1]).then_inc(s_simT, 1)

            def exps(b):
                act.wait_ge(s_sc, b + 1)
                act.activation(ex[:], sc[:], ACT.Exp, scale=float(1.0 / np.sqrt(SD))).then_inc(s_ex, 1)

            def evac_ao(b):
                act.wait_ge(s_aoT, b + 1)
                act.activation(aoT[:, ds(b * S, S)], ps_one[0:SK, 0:S], ACT.Copy).then_inc(s_aoTs, 1)

            def run(b, par, post, prep):
                steps = {}
                if post:
                    steps = {0: [lambda: evac_sim(b - 1)], 9: [lambda: exps(b - 1)], 12: [lambda: evac_ao(b - 1)]}
                if prep:
                    steps[2] = [lambda: evac_x(b + 1)]
                    steps[4] = [lambda: evac_h(b + 1, 1 - par)]
                if isinstance(b, int) and b == B:
                    for g in sorted(steps):
                        for step in steps[g]:
                            step()
                    return

                def relus(g):
                    if g == 0:
                        act.wait_ge(s_hn, b + 1)
                        act.wait_ge(s_hb, b + 1)
                    if g >= 2 or not isinstance(b, int) or b > 0:
                        act.wait_ge(s_mm1, NG * b + g - 1)
                    for r in range(DV, GI):
                        i = GI * g + r
                        ins = act.activation(pair[:, g % 2, r * S:(r + 1) * S], hn[:, par, :], ACT.Relu,
                                             bias=hb[:, par, i:i + 1])
                    ins.then_inc(s_paira, 1)
                    act.wait_ge(s_mm1, NG * b + g + 1)
                    if g >= 2 or not isinstance(b, int) or b > 0:
                        act.wait_ge(s_mm2, NG * b + g - 1)
                    act.activation(u[:, g % 2, :], ps_u[:, g % 2, 0:GI // 2 * S], ACT.Relu,
                                   bias=b2[:, 0:1]).then_inc(s_u, 1)
                schedule(steps, relus)

            act.wait_ge(s_in, LOADED)
            evac_x(0)
            evac_h(0, 0)
            batches(act, run)

        @block.tensor
        def _(pe):
            pe.wait_ge(s_in, LOADED)

            def transpose_x(b):
                pe.wait_ge(s_xn, b + 1)
                if not isinstance(b, int) or b > 0:
                    pe.wait_ge(s_xnT, DC * b)
                for c in range(DC):
                    ins = pe.transpose(ps_xT[:, c, 0:S], xn[:, c * P:(c + 1) * P], ident[0:S, 0:S])
                ins.then_inc(s_xT, 1)

            def hqkv(b):
                pe.wait_ge(s_xnT, DC * (b + 1))
                if not isinstance(b, int) or b > 0:
                    pe.wait_ge(s_kvp, b)
                for c in range(DC):
                    pe.matmul(ps_hq[:, 0:S], w1[:, c, :], xnT[:, c, :], start=(c == 0), stop=(c == DC - 1))
                for c in range(DC):
                    ins = pe.matmul(ps_hq[0:S, 256:256 + 3 * SK], xnT[:, c, :], wqkv[:, c, :],
                                    start=(c == 0), stop=(c == DC - 1))
                ins.then_inc(s_hq, 1)

            def layer3(b, g):
                pe.wait_ge(s_u, NG * b + g + 1)
                if g == 0 and (not isinstance(b, int) or b > 0):
                    pe.wait_ge(s_simT, b)
                for r in range(GI // 2):
                    at = GI * g + r
                    ins = pe.matmul(ps_simT[:, at:at + GI // 2 + 1:GI // 2], u[:, g % 2, r * S:(r + 1) * S],
                                    w3[:], start=True, stop=True)
                ins.then_inc(s_mm2, 1)

            def sim_back(b):
                pe.wait_ge(s_simT, b + 1)
                if not isinstance(b, int) or b > 0:
                    pe.wait_ge(s_aoTs, b)
                pe.transpose(ps_one[0:S, 0:S], simT[:], ident[0:S, 0:S]).then_inc(s_sim, 1)

            def mask_back(b):
                pe.wait_ge(s_mask, b + 1)
                pe.transpose(ps_one[:].bitcast(BF16)[0:S, 0:S], mask[:], identb[:]).then_inc(s_mT, 1)

            def count(b):
                pe.wait_ge(s_mTs, b + 1)
                pe.matmul(ps_one[0:S, 0:S], tri[:], maskT[:], start=True, stop=True).then_inc(s_cum, 1)

            def gather(par, lo, signal):
                for t in range(TOP):
                    out = ps_g[:, t // NH1, (t % NH1) * SK:(t % NH1 + 1) * SK]
                    for part in range(3):
                        ins = pe.matmul(out, onehot[:, t, :], kvp[:, par, part, lo:lo + SK],
                                        start=(part == 0), stop=(part == 2))
                ins.then_inc(signal, 1)

            def gather_k(b, par):
                pe.wait_ge(s_oh, b + 1)
                pe.wait_ge(s_kvp, b + 1)
                gather(par, 0, s_gk)

            def gather_v(b, par):
                pe.wait_ge(s_sc, b + 1)
                gather(par, SK, s_gv)

            def ao_back(b):
                pe.wait_ge(s_ao, b + 1)
                pe.transpose(ps_one[:, 0:S], ao[:], ident[0:S, 0:S]).then_inc(s_aoT, 1)

            def run(b, par, post, prep):
                steps = {}
                if post:
                    steps = {1: [lambda: sim_back(b - 1)], 3: [lambda: mask_back(b - 1)], 5: [lambda: count(b - 1)],
                             7: [lambda: gather_k(b - 1, 1 - par)], 9: [lambda: gather_v(b - 1, 1 - par)], 11: [lambda: ao_back(b - 1)]}
                if prep:
                    steps.setdefault(1, []).append(lambda: transpose_x(b + 1))
                    steps.setdefault(3, []).append(lambda: hqkv(b + 1))
                if isinstance(b, int) and b == B:
                    for g in sorted(steps):
                        for step in steps[g]:
                            step()
                    return

                def layer2(g):
                    pe.wait_ge(s_pairv, NG * b + g + 1)
                    pe.wait_ge(s_paira, NG * b + g + 1)
                    if g >= 2 or not isinstance(b, int) or b > 0:
                        pe.wait_ge(s_u, NG * b + g - 1)
                    half = GI // 2 * S
                    for side in range(2):
                        ins = pe.matmul(ps_u[side * F2:(side + 1) * F2, g % 2, 0:half], w2[:],
                                        pair[:, g % 2, side * half:(side + 1) * half], start=True, stop=True)
                    ins.then_inc(s_mm1, 1)
                    if g >= 1:
                        layer3(b, g - 1)
                schedule(steps, layer2, last=lambda: layer3(b, NG - 1))

            transpose_x(0)
            hqkv(0)
            batches(pe, run)


def later(eng, sem, value):
    if not isinstance(value, int) or value > 0:
        eng.wait_ge(sem, value)


def layer_norm_rows(dve, c, y, stats, mv, mean, rstd, var, tmp, s_var, s_sqrt, sqrts):
    for t in range(RT):
        ins = dve.bn_aggr(mv[:, t, :], stats[:, t, :])
    c.link(ins)
    c.link(dve.tensor_copy(mean[:], mv[:, :, 0]))
    dve.tensor_scalar(var[:], mv[:, :, 1], EPS, None, ALU.add).then_inc(s_var, 1)
    dve.wait_ge(s_var, sqrts)
    dve.wait_ge(s_sqrt, sqrts)
    c.link(dve.reciprocal(rstd[:], tmp[:]))
    rstd_newton(dve, c, rstd[:], var[:], tmp[:])


def project_queries(nc, a, aoT, sq, x1_dram, qT_dram):
    with ExitStack() as ctx:
        def sb(name, shape, dt=F32):
            return ctx.enter_context(nc.sbuf_tensor("p2_" + name, shape, dt))

        def pb(name, shape, dt=F32):
            return ctx.enter_context(nc.psum_tensor("p2_" + name, shape, dt))

        def sem(name):
            return ctx.enter_context(nc.semaphore("p2_" + name))

        y = sb("y", [P, RT, D])
        wout, wq = sb("wout", [SK, D]), sb("wq", [P, DC, D])
        bout, bq = sb("bout", [P, D]), sb("bq", [P, D])
        ident, identb = sb("ident", [P, P]), sb("identb", [P, P], BF16)
        stats, mv = sb("stats", [P, RT, 6]), sb("mv", [P, RT, 2])
        mean, rstd, var, tmp = (sb(n, [P, RT]) for n in ("mean", "rstd", "var", "tmp"))
        yT = sb("yT", [P, 2, DC, P])
        qf, qn = sb("qf", [P, H, HD]), sb("qn", [P, H, HD])
        qi = sb("qi", [P, 2, D], BF16)
        am, rq = sb("am", [P, H]), sb("rq", [P, H])
        qT = sb("qT", [P, DC, ROWS], BF16)
        ps_o, ps_t, ps_q = pb("ps_o", [P, 2, D]), pb("ps_t", [P, 2, DC, P]), pb("ps_q", [P, 2, D])
        ps_i = pb("ps_i", [P, 2, 2 * D], BF16)
        names = "in o y var sqrt x1 c t tT q qi i qT st"
        s = {n: sem("s_" + n) for n in names.split()}
        loads = [
            (y[:], a["x"].rearrange("b s d -> (b s) d").rearrange("(t p) d -> p t d", p=P)),
            (wout[:], a["WoutT"]), (wq[:], a["Wq"].rearrange("(c p) n -> p c n", p=P)),
            (bout[:], a["bout"].rearrange("(o n) -> o n", o=1).broadcast_to([P, D])),
            (bq[:], a["bq"].rearrange("(o n) -> o n", o=1).broadcast_to([P, D])),
            (ident[:], a["ident"]), (identb[:], a["identb"]),
        ]
        LOADED = 16 * len(loads)
        SCALE = float(1.0 / np.sqrt(HD))
        block = ctx.enter_context(nc.Block())

        @block.sync
        def _(sp):
            for out, src in loads:
                sp.dma_start(out, src).then_inc(s["in"], 16)
            sp.wait_ge(s["x1"], RT)
            sp.dma_start(x1_dram.rearrange("(t p) d -> p t d", p=P), y[:]).then_inc(s["st"], 16)
            sp.wait_ge(s["qT"], RT)
            sp.dma_start(qT_dram.rearrange("(c p) n -> p c n", p=P), qT[:]).then_inc(s["st"], 16)
            sp.wait_ge(s["st"], 32)

        @block.tensor
        def _(pe):
            pe.wait_ge(s["in"], LOADED)
            for t in range(RT):
                later(pe, s["y"], t - 1)
                pe.matmul(ps_o[:, t % 2, :], aoT[:, t * P:(t + 1) * P], wout[:], start=True, stop=True)\
                    .then_inc(s["o"], 1)

            def queries(t):
                pe.wait_ge(s["tT"], t + 1)
                later(pe, s["q"], t - 1)
                for c in range(DC):
                    ins = pe.matmul(ps_q[:, t % 2, :], yT[:, t % 2, c, :], wq[:, c, :], start=(c == 0),
                                    stop=(c == DC - 1))
                ins.then_inc(s["c"], 1)

            def turn(t):
                pe.wait_ge(s["qi"], t + 1)
                later(pe, s["qT"], t - 1)
                for c in range(DC):
                    ins = pe.transpose(ps_i[:, t % 2, c * P:(c + 1) * P], qi[:, t % 2, c * P:(c + 1) * P], identb[:])
                ins.then_inc(s["i"], 1)

            for t in range(RT + 2):
                if t < RT:
                    pe.wait_ge(s["x1"], t + 1)
                    later(pe, s["tT"], t - 1)
                    for c in range(DC):
                        ins = pe.transpose(ps_t[:, t % 2, c, :], y[:, t, c * P:(c + 1) * P], ident[:])
                    ins.then_inc(s["t"], 1)
                if 1 <= t <= RT:
                    queries(t - 1)
                if t >= 2:
                    turn(t - 2)

        @block.scalar
        def _(act):
            act.wait_ge(s["var"], 1)
            act.activation(tmp[:], var[:], ACT.Sqrt).then_inc(s["sqrt"], 1)
            for t in range(RT + 2):
                if t < RT:
                    act.wait_ge(s["t"], t + 1)
                    later(act, s["c"], t - 1)
                    act.activation(yT[:, t % 2, :, :], ps_t[:, t % 2, :, :], ACT.Copy).then_inc(s["tT"], 1)
                if t >= 2:
                    u = t - 2
                    act.wait_ge(s["i"], u + 1)
                    act.activation(qT[:, :, u * P:(u + 1) * P], ps_i[:, u % 2, 0:D].rearrange("p (c n) -> p c n", c=DC),
                                   ACT.Copy).then_inc(s["qT"], 1)

        @block.vector
        def _(dve):
            c = Chain(dve, sem("s_chain"))
            dve.wait_ge(s["in"], LOADED)
            for t in range(RT):
                dve.wait_ge(s["o"], t + 1)
                c.link(dve.scalar_tensor_tensor(y[:, t, :], y[:, t, :], 2.0, ps_o[:, t % 2, :], ALU.mult, ALU.add))
                dve.tensor_tensor(y[:, t, :], y[:, t, :], bout[:], ALU.add).then_inc(s["y"], 1)
                dve.wait_ge(s["y"], t + 1)
                ins = dve.bn_stats(stats[:, t, :], y[:, t, :])
            c.link(ins)
            layer_norm_rows(dve, c, y, stats, mv, mean, rstd, var, tmp, s["var"], s["sqrt"], 1)
            for t in range(RT):
                dve.tensor_scalar(y[:, t, :], y[:, t, :], mean[:, t:t + 1], rstd[:, t:t + 1], ALU.subtract, ALU.mult)\
                   .then_inc(s["x1"], 1)
            for t in range(RT):
                dve.wait_ge(s["c"], t + 1)
                dve.tensor_tensor(qf[:].rearrange("p h d -> p (h d)"), ps_q[:, t % 2, :], bq[:], ALU.add)\
                   .then_inc(s["q"], 1)
                dve.wait_ge(s["q"], t + 1)
                c.link(dve.tensor_reduce(am[:], qf[:], X, ALU.max, apply_absolute_value=True))
                c.link(dve.tensor_scalar(sq[:, :, t], am[:], SCALE / 127.0, 1e-8, ALU.mult, ALU.max))
                c.link(dve.reciprocal(rq[:], sq[:, :, t]))
                c.link(dve.tensor_scalar(rq[:], rq[:], SCALE, None, ALU.mult))
                c.link(dve.tensor_tensor(qn[:], qf[:], rq[:].unsqueeze(2).broadcast_to([P, H, HD]), ALU.mult))
                later(dve, s["i"], t - 1)
                dve.tensor_scalar(qi[:, t % 2, :], qn[:].rearrange("p h d -> p (h d)"), MAGIC, MAGIC,
                                  ALU.add, ALU.subtract).then_inc(s["qi"], 1)


def project_keys(nc, a, svr, kT_dram, v_dram, vi_dram):
    with ExitStack() as ctx:
        def sb(name, shape, dt=F32):
            return ctx.enter_context(nc.sbuf_tensor("p3_" + name, shape, dt))

        def pb(name, shape, dt=F32):
            return ctx.enter_context(nc.psum_tensor("p3_" + name, shape, dt))

        def sem(name):
            return ctx.enter_context(nc.semaphore("p3_" + name))

        R = 4
        CH = 2 * KT
        wkv = sb("wkv", [P, DC, 2 * D])
        bk, bv = sb("bk", [KT, D]), sb("bv", [KT, D])
        identb = sb("identb", [P, P], BF16)
        ctxT = sb("ctxT", [P, 2, DC, CH])
        kf, kn = sb("kf", [KT, H, HD]), sb("kn", [KT, H, HD])
        am, sk, rk = sb("am", [KT, H]), sb("sk", [KT, H]), sb("rk", [KT, H])
        kd = sb("kd", [KT, R, D])
        kd2 = sb("kd2", [KT, 2, D])
        kd3 = sb("kd3", [KT, 2, D])
        part = sb("part", [KT, R, 3, D], BF16)
        kTs = sb("kTs", [P, 2, DC * 3, CH], BF16)
        vf = sb("vf", [KT, R, D])
        vmax, vall = sb("vmax", [P, D]), sb("vall", [P, D])
        rv = sb("rv", [P, D])
        VC = 4
        vl, vn = sb("vl", [KT, 2, VC * D]), sb("vn", [KT, 2, VC * D])
        vi = sb("vi", [KT, 2, H, VC, HD], BF16)
        ps_k, ps_v = pb("ps_k", [KT, 2, D]), pb("ps_v", [KT, 2, D])
        ps_T = pb("ps_T", [P, 2, 16, P], BF16)
        s = {n: sem("s_" + n) for n in ("in ctx k v kf vf kd h m l r2 r3 T ev kst vst0 vst1 chain vmax vmz vr vl0 vl1 vi vn vist "
                                        "chain2").split()}
        s_ctx = [s["ctx"], sem("s_ctx1")]
        s_kst = [s["kst"], sem("s_kst1")]
        s_vst = [sem(f"s_vst_{i}") for i in range(R)]
        s_vl = [s["vl0"], s["vl1"]]
        s_vist = [s["vist"], sem("s_vist1")]
        loads = [
            (wkv[:], a["Wkv"].rearrange("(c p) n -> p c n", p=P)),
            (bk[:], a["bkv"][0:D].rearrange("(o n) -> o n", o=1).broadcast_to([KT, D])),
            (bv[:], a["bkv"][D:2 * D].rearrange("(o n) -> o n", o=1).broadcast_to([KT, D])),
            (identb[:], a["identb"]),
        ]
        LOADED = 16 * len(loads)
        NCH = NKT // 2
        ctxT_d = a["ctxT"].rearrange("(c p) n -> p c n", p=P)
        LAG = 3

        def steps(eng, step):
            for j in range(R):
                step(j, j)
            with eng.Fori(1, NKT // R) as k:
                for r in range(R):
                    step(k * R + r, r)
            for j in range(NKT, NKT + LAG):
                step(j, j % R)

        def first(j):
            return isinstance(j, int) and j < R

        def over(j):
            return isinstance(j, int) and j >= NKT

        def has(j, lag):
            return not (isinstance(j, int) and (j < lag or j - lag >= NKT))

        block = ctx.enter_context(nc.Block())

        @block.sync
        def _(sp):
            for out, src in loads:
                sp.dma_start(out, src).then_inc(s["in"], 16)

            def load(ch, half):
                later(sp, s["v"], 2 * (ch - 1))
                sp.dma_start(ctxT[:, half, :, :], ctxT_d[:, :, ds(ch * CH, CH)]).then_inc(s_ctx[half], 16)

            def store_v(ch, half):
                for sub in range(2):
                    sp.wait_ge(s["vf"], 2 * ch + sub + 1)
                    sp.dma_start(v_dram[ds((2 * ch + sub) * KT, KT), :], vf[:, 2 * half + sub, :])\
                      .then_inc(s_vst[2 * half + sub], 16)

            def store_k(ch, half):
                sp.wait_ge(s["ev"], 2 * (ch + 1))
                dst = kT_dram.rearrange("a (c p) n -> p c a n", p=P)
                for c in range(DC):
                    sp.dma_start(dst[:, c, :, ds(ch * CH, CH)], kTs[:, half, c * 3:(c + 1) * 3, :])\
                      .then_inc(s_kst[half], 16)

            load(0, 0)
            load(1, 1)
            for ch in range(2):
                load(ch + 2, ch)
                store_v(ch, ch)
            with sp.Fori(1, NCH // 2 - 1) as k:
                for half in range(2):
                    load(2 * k + 2 + half, half)
                    store_v(2 * k + half, half)
                    store_k(2 * k - 2 + half, half)
            for half in range(2):
                store_v(NCH - 2 + half, half)
                store_k(NCH - 4 + half, half)
            for half in range(2):
                store_k(NCH - 2 + half, half)
            for half in range(2):
                sp.wait_ge(s_kst[half], 16 * DC * NCH // 2)

            for r in range(R):
                sp.wait_ge(s_vst[r], 16 * NKT // R)
            vd = v_dram.rearrange("(j p) d -> p j d", p=KT)
            vid = vi_dram.rearrange("h p (j d) -> p h j d", d=HD)

            def load_v(c, half):
                later(sp, s["vn"], c - 1)
                sp.dma_start(vl[:, half, :].rearrange("p (j d) -> p j d", j=VC), vd[:, ds(c * VC, VC), :])\
                    .then_inc(s_vl[half], 16)

            def store_vi(c, half):
                sp.wait_ge(s["vi"], c + 1)
                sp.dma_start(vid[:, :, ds(c * VC, VC), :], vi[:, half, :, :, :]).then_inc(s_vist[half], 16)
            NV = NKT // VC
            load_v(0, 0)
            load_v(1, 1)
            with sp.Fori(0, NV // 2 - 1) as k:
                for half in range(2):
                    load_v(2 * k + 2 + half, half)
                    store_vi(2 * k + half, half)
            for half in range(2):
                store_vi(NV - 2 + half, half)
            for half in range(2):
                sp.wait_ge(s_vist[half], 16 * NV // 2)

        @block.gpsimd
        def _(pool):
            def step(j, r):
                if has(j, 0):
                    pool.wait_ge(s["h"], j + 1)
                    later(pool, s["m"], j - 1)
                    later(pool, s["r3"], j - 1)
                    pool.tensor_tensor(kd2[:, r % 2, :], kd[:, r, :], part[:, r, 0, :], ALU.subtract)\
                        .then_inc(s["r2"], 1)
                if has(j, 1):
                    pool.wait_ge(s["m"], j)
                    pool.wait_ge(s["r2"], j)
                    later(pool, s["l"], j - 2)
                    pool.tensor_tensor(kd3[:, (r - 1) % 2, :], kd2[:, (r - 1) % 2, :], part[:, (r - 1) % R, 1, :],
                                       ALU.subtract).then_inc(s["r3"], 1)
            steps(pool, step)
            pool.wait_ge(s["vmax"], NKT)
            pool.partition_all_reduce(vall[:], vmax[:], P, bass.bass_isa.ReduceOp.max).then_inc(s["vr"], 1)

        @block.tensor
        def _(pe):
            pe.wait_ge(s["in"], LOADED)

            def step(j, r):
                if has(j, 0):
                    half, sub = r // 2, r % 2
                    pe.wait_ge(s_ctx[half], 16 * (j // R + 1) if isinstance(j, int) else 16 * (quotient[0] + 1))
                    for w, (ps, done, used) in enumerate(((ps_k, s["k"], s["kf"]), (ps_v, s["v"], s["vf"]))):
                        later(pe, used, j - 1)
                        for c in range(DC):
                            ins = pe.matmul(ps[:, r % 2, :], ctxT[:, half, c, sub * KT:(sub + 1) * KT],
                                            wkv[:, c, w * D:(w + 1) * D], start=(c == 0), stop=(c == DC - 1))
                        ins.then_inc(done, 1)
                if has(j, LAG):
                    o = (r - LAG) % R
                    pe.wait_ge(s["l"], j - LAG + 1)
                    later(pe, s["ev"], j - LAG)
                    for c in range(DC):
                        for n in range(3):
                            ins = pe.transpose(ps_T[:, (c * 3 + n) // 8, (c * 3 + n) % 8, 0:KT],
                                               part[:, o, n, c * P:(c + 1) * P], identb[0:KT, 0:KT])
                    ins.then_inc(s["T"], 1)

            quotient = [0]
            for j in range(R):
                step(j, j)
            with pe.Fori(1, NKT // R) as k:
                quotient[0] = k
                for r in range(R):
                    step(k * R + r, r)
            for j in range(NKT, NKT + LAG):
                step(j, j % R)

        @block.scalar
        def _(act):
            def step(j, r):
                if has(j, 0):
                    act.wait_ge(s["kd"], j + 1)
                    later(act, s["T"], j - R + 1)
                    act.activation(part[:, r, 0, :], kd[:, r, :], ACT.Copy).then_inc(s["h"], 1)
                if has(j, 1):
                    act.wait_ge(s["r2"], j)
                    act.activation(part[:, (r - 1) % R, 1, :], kd2[:, (r - 1) % 2, :], ACT.Copy).then_inc(s["m"], 1)
                if has(j, 2):
                    act.wait_ge(s["r3"], j - 1)
                    act.activation(part[:, (r - 2) % R, 2, :], kd3[:, (r - 2) % 2, :], ACT.Copy).then_inc(s["l"], 1)
                if has(j, LAG):
                    o = (r - LAG) % R
                    act.wait_ge(s["T"], j - LAG + 1)
                    if not (isinstance(j, int) and j - LAG < R):
                        if isinstance(j, int):
                            act.wait_ge(s_kst[o // 2], 16 * DC * ((j - LAG) // R))
                        else:
                            act.wait_ge(s_kst[o // 2], 16 * DC * (quotient[0] if r >= LAG else quotient[0] - 1))
                    for b, n in ((0, 8), (1, 4)):
                        ins = act.activation(kTs[:, o // 2, b * 8:b * 8 + n, (o % 2) * KT:(o % 2 + 1) * KT],
                                             ps_T[:, b, 0:n, 0:KT], ACT.Copy)
                    ins.then_inc(s["ev"], 1)

            quotient = [0]
            for j in range(R):
                step(j, j)
            for j in range(R, 2 * R):
                step(j, j % R)
            with act.Fori(2, NKT // R) as k:
                quotient[0] = k
                for r in range(R):
                    step(k * R + r, r)
            for j in range(NKT, NKT + LAG):
                step(j, j % R)

        @block.vector
        def _(dve):
            dve.memset(vmax[:], 0.0).then_inc(s["vmz"], 1)
            dve.wait_ge(s["in"], LOADED)
            dve.wait_ge(s["vmz"], 1)
            LINKS = 6

            def tile(j, r):
                c = Chain(dve, s["chain"], LINKS * j)
                dve.wait_ge(s["k"], j + 1)
                dve.tensor_tensor(kf[:].rearrange("p h d -> p (h d)"), ps_k[:, r % 2, :], bk[:], ALU.add)\
                   .then_inc(s["kf"], 1)
                dve.wait_ge(s["v"], j + 1)
                if quotient[0] is not None:
                    dve.wait_ge(s_vst[r], 16 * quotient[0])
                dve.tensor_tensor(vf[:, r, :], ps_v[:, r % 2, :], bv[:], ALU.add).then_inc(s["vf"], 1)
                dve.wait_ge(s["kf"], j + 1)
                c.link(dve.tensor_reduce(am[:], kf[:], X, ALU.max, apply_absolute_value=True))
                c.link(dve.tensor_scalar(sk[:], am[:], 1.0 / 127.0, 1e-8, ALU.mult, ALU.max))
                c.link(dve.reciprocal(rk[:], sk[:]))
                c.link(dve.tensor_tensor(kn[:], kf[:], rk[:].unsqueeze(2).broadcast_to([KT, H, HD]), ALU.mult))
                dve.wait_ge(s["vf"], j + 1)
                c.link(dve.scalar_tensor_tensor(vmax[0:KT, :], vf[:, r, :], -1.0, vmax[0:KT, :], ALU.mult, ALU.max))
                c.link(dve.tensor_scalar(kn[:], kn[:], MAGIC, MAGIC, ALU.add, ALU.subtract))
                dve.tensor_tensor(vmax[0:KT, :], vmax[0:KT, :], vf[:, r, :], ALU.max).then_inc(s["vmax"], 1)
                if quotient[0] is not None:
                    dve.wait_ge(s["r2"], j - R + 1)
                dve.tensor_tensor(kd[:, r, :].rearrange("p (h d) -> p h d", h=H), kn[:],
                                  sk[:].unsqueeze(2).broadcast_to([KT, H, HD]), ALU.mult).then_inc(s["kd"], 1)

            quotient = [None]
            for j in range(R):
                tile(j, j)
            with dve.Fori(1, NKT // R) as k:
                quotient[0] = k
                for r in range(R):
                    tile(k * R + r, r)
            c = Chain(dve, s["chain2"])
            dve.wait_ge(s["vr"], 1)
            c.link(dve.tensor_scalar(svr[:], vall[:], 1.0 / 127.0, 1e-8, ALU.mult, ALU.max))
            c.link(dve.reciprocal(rv[:], svr[:]))

            def chunk(q, half, k, sub):
                dve.wait_ge(s_vl[half], 16 * (k + 1))
                later(dve, s["vi"], q - 1)
                dve.tensor_tensor(vn[:, half, :].rearrange("p (j d) -> p j d", j=VC),
                                  vl[:, half, :].rearrange("p (j d) -> p j d", j=VC),
                                  rv[0:KT, :].unsqueeze(1).broadcast_to([KT, VC, D]), ALU.mult).then_inc(s["vn"], 1)
                dve.wait_ge(s["vn"], q + 1)
                if not isinstance(k, int) or k > 0:
                    dve.wait_ge(s_vist[half], 16 * k)
                for t in range(VC):
                    ins = dve.tensor_scalar(vi[:, half, :, t, :],
                                            vn[:, half, t * D:(t + 1) * D].rearrange("p (h d) -> p h d", d=HD),
                                            MAGIC, MAGIC, ALU.add, ALU.subtract)
                ins.then_inc(s["vi"], 1)
            for half in range(2):
                chunk(half, half, 0, half)
            with dve.Fori(1, NKT // VC // 2) as k:
                for half in range(2):
                    chunk(2 * k + half, half, k, half)


def cross_attention(nc, a, sq, svr, xo, qT_dram, kT_dram, vi_dram):
    with ExitStack() as ctx:
        def sb(name, shape, dt=F32):
            return ctx.enter_context(nc.sbuf_tensor("p4_" + name, shape, dt))

        def pb(name, shape, dt=F32):
            return ctx.enter_context(nc.psum_tensor("p4_" + name, shape, dt))

        def sem(name):
            return ctx.enter_context(nc.semaphore("p4_" + name))

        SG = 6
        GW = KEYS // SG
        MW = GW // 2
        NB = 6
        TB = NKT // NB
        EP = KEYS // NEXP
        LN255 = float(np.log(255.0))

        kT = sb("kT", [3 * HD, 2, KEYS], BF16)
        qs = sb("qs", [3 * HD, 2, ROWS], BF16)
        vh = sb("vh", [KT, 2, NKT * HD], BF16)
        nsq = sb("nsq", [P, H * RT])
        sc = sb("sc", [P, 2, KEYS])
        e = sb("e", [P, KEYS], U16)
        et = sb("et", [KT, NB, TB * P], BF16)
        top = sb("top", [P, 2, SG])
        mx, bias = sb("mx", [P, 2]), sb("bias", [P, 2])
        sums = sb("sums", [P, 2, RT * NEXP])
        den, rden = sb("den", [P, RT]), sb("rden", [P, RT])
        on = sb("on", [P, RT, HD])
        identb = sb("identb", [P, P], BF16)
        ps_s = pb("ps_s", [P, 2, 2, 512])
        ps_t = pb("ps_t", [KT, 2, TB * P], BF16)
        ps_o = pb("ps_o", [P, 2, 512])
        s = {n: sem("s_" + n) for n in "id turn nsq qk copy top bias exp T evd eva pv chain norm".split()}
        s_kq, s_v = [sem("s_kq0"), sem("s_kq1")], [sem("s_v0"), sem("s_v1")]
        ND = 6

        block = ctx.enter_context(nc.Block())

        @block.sync
        def _(sp):
            sp.dma_start(identb[:], a["identb"]).then_inc(s["id"], 16)

            def load(h, hp):
                if not isinstance(h, int) or h >= 2:
                    sp.wait_ge(s["qk"], SG * RT * (h - 1))
                for part in range(3):
                    sp.dma_start(kT[part * HD:(part + 1) * HD, hp, :], kT_dram[part, ds(h * HD, HD), :])\
                      .then_inc(s_kq[hp], 16)
                    sp.dma_start(qs[part * HD:(part + 1) * HD, hp, :], qT_dram[ds(h * HD, HD), :])\
                      .then_inc(s_kq[hp], 16)
                if not isinstance(h, int) or h >= 2:
                    sp.wait_ge(s["pv"], NB + NB * RT * (h - 1))
                sp.dma_start(vh[:, hp, :], vi_dram[ds(h, 1), :, :].rearrange("h p n -> p (h n)")).then_inc(s_v[hp], 16)
            load(0, 0)
            load(1, 1)
            with sp.Fori(1, H // 2) as k:
                for hp in range(2):
                    load(2 * k + hp, hp)

        def heads(eng, first, step, finish):
            first()
            step(0, 0, 0, 0, 0)

            def head(k, hp, last):
                base = RT * (2 * k + hp)
                with eng.Fori(0, (RT - 2) // 2) as m:
                    for half in range(2):
                        step(base + 2 * m + 1 + half, 2 * m + 1 + half, 1 - half, hp, k)
                step(base + RT - 1, RT - 1, 1, hp, k, last=last)
                if not last:
                    step(base + RT, 0, 0, 1 - hp, k + hp)
            with eng.Fori(0, H // 2 - 1) as k:
                head(k, 0, False)
                head(k, 1, False)
            head(H // 2 - 1, 0, False)
            head(H // 2 - 1, 1, True)
            finish()

        @block.tensor
        def _(pe):
            pe.sem_inc(s["pv"], NB)
            pe.wait_ge(s["id"], 16)

            def products(n, g, t, hp, k):
                if g == 0 and isinstance(t, int) and t == 0:
                    pe.wait_ge(s_kq[hp], 16 * ND * (k + 1))
                later(pe, s["copy"], SG * n + g - 1)
                for b in range(2):
                    ins = pe.matmul(ps_s[:, g % 2, b, 0:MW], qs[:, hp, ds(t * P, P)],
                                    kT[:, hp, g * GW + b * MW:g * GW + (b + 1) * MW], start=True, stop=True)
                ins.then_inc(s["qk"], 1)

            def turn(n, i):
                pe.wait_ge(s["exp"], NEXP * n + i * NEXP // NB + 1)
                later(pe, s["evd"] if i % 2 == 0 else s["eva"], NB // 2 * n + i // 2)
                for j in range(TB):
                    at = (i * TB + j) * KT
                    ins = pe.transpose(ps_t[:, i % 2, j * P:(j + 1) * P], e[:, at:at + KT].bitcast(BF16), identb[:])
                ins.then_inc(s["T"], 1)

            def attend(n, i, t, hp, k):
                pe.wait_ge(s["evd"] if i % 2 == 0 else s["eva"], NB // 2 * n + i // 2 + 1)
                if i == 0 and isinstance(t, int) and t == 0:
                    pe.wait_ge(s_v[hp], 16 * (k + 1))
                    later(pe, s["norm"], 2 * k + hp)
                for j in range(TB):
                    ins = pe.matmul(ps_o[:, hp, ds(t * HD, HD)], et[:, i, j * P:(j + 1) * P],
                                    vh[:, hp, (i * TB + j) * HD:(i * TB + j + 1) * HD],
                                    start=(i == 0 and j == 0), stop=(i == NB - 1 and j == TB - 1))
                ins.then_inc(s["pv"], 1)

            def step(n, t, par, hp, k, last=False):
                if isinstance(t, int) and t == RT - 1:
                    nxt = (0, 1 - hp, k + hp)
                else:
                    nxt = (t + 1, hp, k)
                before = (t - 1, hp, k) if not (isinstance(t, int) and t == 0) else (RT - 1, 1 - hp, k + hp - 1)
                start = isinstance(n, int) and n == 0
                for g in range(SG):
                    if not last:
                        products(n + 1, g, *nxt)
                    if g == 0:
                        if not start:
                            turn(n - 1, NB - 1)
                            attend(n - 1, NB - 2, *before)
                    else:
                        turn(n, g - 1)
                        if g == 1:
                            if not start:
                                attend(n - 1, NB - 1, *before)
                        else:
                            attend(n, g - 2, t, hp, k)

            def first():
                for g in range(SG):
                    products(0, g, 0, 0, 0)

            def finish():
                n, at = H * RT - 1, (RT - 1, 1, H // 2 - 1)
                turn(n, NB - 1)
                attend(n, NB - 2, *at)
                attend(n, NB - 1, *at)
            heads(pe, first, step, finish)

        @block.scalar
        def _(act):
            act.preload_act_table(ACT.Exp)
            act.wait_ge(s["nsq"], 1)

            def evac(n, i):
                act.wait_ge(s["T"], NB * n + i + 1)
                act.wait_ge(s["pv"], NB * n + i + 1)
                act.activation(et[:, i, :], ps_t[:, i % 2, :].bitcast(U16), ACT.Copy).then_inc(s["eva"], 1)

            def step(n, t, par, hp, k, last=False):
                for part in range(NEXP):
                    if part == 0:
                        act.wait_ge(s["bias"], n + 1)
                    later(act, s["T"], NB * (n - 1) + (part + 1) * NB // NEXP)
                    act.sem_inc(s["turn"], 1)
                    act.activation(e[:, part * EP:(part + 1) * EP], sc[:, par, part * EP:(part + 1) * EP], ACT.Exp,
                                   bias=bias[:, par:par + 1], scale=sq[:].rearrange("p h t -> p (h t)")[:, ds(n, 1)],
                                   accum_out=sums[:, hp, ds(t * NEXP + part, 1)]).then_inc(s["exp"], 1)
                    if part == 0:
                        if not (isinstance(n, int) and n == 0):
                            evac(n - 1, NB - 1)
                    else:
                        evac(n, 2 * part - 1)

            def finish():
                evac(H * RT - 1, NB - 1)
            heads(act, lambda: None, step, finish)

        @block.vector
        def _(dve):
            dve.tensor_scalar(nsq[:], sq[:].rearrange("p h t -> p (h t)"), -1.0, None, ALU.mult).then_inc(s["nsq"], 1)
            dve.wait_ge(s["nsq"], 1)

            def copies(n, g, par):
                if g == 0:
                    later(dve, s["exp"], NEXP * (n - 1))
                dve.wait_ge(s["qk"], SG * n + g + 1)
                dve.tensor_scalar(sc[:, par, g * GW:(g + 1) * GW].rearrange("p (b n) -> p b n", b=2),
                                  ps_s[:, g % 2, :, 0:MW], 1.0, None, ALU.mult, ALU.max,
                                  accum_out=top[:, par, g:g + 1]).then_inc(s["copy"], 1)

            def biases(n, par):
                dve.wait_ge(s["copy"], SG * (n + 1))
                dve.tensor_reduce(mx[:, par:par + 1], top[:, par, :], X, ALU.max).then_inc(s["top"], 1)
                dve.wait_ge(s["top"], n + 1)
                dve.tensor_scalar(bias[:, par:par + 1], mx[:, par:par + 1], nsq[:, ds(n, 1)], LN255,
                                  ALU.mult, ALU.add).then_inc(s["bias"], 1)

            def evac(n, i):
                dve.wait_ge(s["T"], NB * n + i + 1)
                dve.wait_ge(s["pv"], NB * n + i + 1)
                dve.tensor_copy(et[:, i, :], ps_t[:, i % 2, :].bitcast(U16)).then_inc(s["evd"], 1)

            def normalise(h, hp):
                dve.wait_ge(s["pv"], NB + NB * RT * (h + 1))
                ch = Chain(dve, s["chain"], 3 * h)
                ch.link(dve.tensor_reduce(den[:], sums[:, hp, :].rearrange("p (t n) -> p t n", n=NEXP), X, ALU.add))
                ch.link(dve.reciprocal(rden[:], den[:]))
                ch.link(dve.tensor_tensor(on[:], ps_o[:, hp, 0:RT * HD].rearrange("p (t d) -> p t d", d=HD),
                                          rden[:].unsqueeze(2).broadcast_to([P, RT, HD]), ALU.mult))
                dve.tensor_tensor(xo[:, :, ds(h * HD, HD)], on[:],
                                  svr[:, ds(h * HD, HD)].unsqueeze(1).broadcast_to([P, RT, HD]), ALU.mult)\
                   .then_inc(s["norm"], 1)

            def step(n, t, par, hp, k, last=False):
                start = isinstance(n, int) and n == 0
                for g in range(SG):
                    if not last:
                        copies(n + 1, g, 1 - par)
                    if g == 0 and not start:
                        evac(n - 1, NB - 2)
                    if g in (2, 4):
                        evac(n, g - 2)
                    if g == 4 and isinstance(t, int) and t == 0 and not start:
                        normalise(2 * k + hp - 1, 1 - hp)
                if not last:
                    biases(n + 1, 1 - par)

            def first():
                for g in range(SG):
                    copies(0, g, 0)
                biases(0, 0)

            def finish():
                evac(H * RT - 1, NB - 2)
                normalise(H - 1, 1)
            dve.memset(den[:], 1.0).then_inc(s["norm"], 1)
            heads(dve, first, step, finish)


LOW = 2.0 ** -12


def output_projection(nc, a, xo, y, t1, t2, t3, xh, xl, x1_dram):
    with ExitStack() as ctx:
        def sb(name, shape, dt=F32):
            return ctx.enter_context(nc.sbuf_tensor("p5_" + name, shape, dt))

        def pb(name, shape, dt=F32):
            return ctx.enter_context(nc.psum_tensor("p5_" + name, shape, dt))

        def sem(name):
            return ctx.enter_context(nc.semaphore("p5_" + name))

        wp, bp = sb("wp", [P, DC, D]), sb("bp", [P, D])
        ident = sb("ident", [P, P])
        raw = sb("raw", [P, DC * FFN])
        mass, total, thr = sb("mass", [P, 3]), sb("total", [P, 3]), sb("thr", [P, 2, 3])
        stats, mv = sb("stats", [P, RT, 6]), sb("mv", [P, RT, 2])
        mean, rstd, var, tmp = (sb(n, [P, RT]) for n in ("mean", "rstd", "var", "tmp"))
        yT = sb("yT", [P, 2, DC, P])
        rest = sb("rest", [P, 2, DC, P])
        ps_t, ps_o = pb("ps_t", [P, 2, DC, P]), pb("ps_o", [P, 2, D])
        s = {n: sem("s_" + n) for n in "in raw x t tT o y var sqrt n xt xh xr xl mass total tern chain".split()}
        WD = [a["w1T"].rearrange("(c p) n -> p c n", p=P), a["w2T"].rearrange("(c p) n -> p c n", p=P),
              a["w3T"].rearrange("(c p) n -> p c n", p=P)]
        block = ctx.enter_context(nc.Block())

        @block.sync
        def _(sp):
            sp.dma_start(wp[:], a["Wp"].rearrange("(c p) n -> p c n", p=P)).then_inc(s["in"], 16)
            sp.dma_start(bp[:], a["bp"].rearrange("(o n) -> o n", o=1).broadcast_to([P, D])).then_inc(s["in"], 16)
            sp.dma_start(ident[:], a["ident"]).then_inc(s["in"], 16)
            sp.dma_start(y[:], x1_dram.rearrange("(t p) d -> p t d", p=P)).then_inc(s["x"], 16)
            for i, w in enumerate(WD):
                later(sp, s["tern"], i)
                sp.dma_start(raw[:].rearrange("p (c n) -> p c n", c=w.shape[1]), w).then_inc(s["raw"], 16)

        @block.gpsimd
        def _(pool):
            for i in range(3):
                pool.wait_ge(s["mass"], i + 1)
                pool.partition_all_reduce(total[:, i:i + 1], mass[:, i:i + 1], P, bass.bass_isa.ReduceOp.add)\
                    .then_inc(s["total"], 1)

        @block.tensor
        def _(pe):
            pe.wait_ge(s["in"], 48)
            for t in range(RT + 1):
                if t < RT:
                    later(pe, s["tT"], t - 1)
                    for c in range(DC):
                        ins = pe.transpose(ps_t[:, t % 2, c, :], xo[:, t, c * P:(c + 1) * P], ident[:])
                    ins.then_inc(s["t"], 1)
                if t >= 1:
                    u = t - 1
                    pe.wait_ge(s["tT"], u + 1)
                    later(pe, s["y"], u - 1)
                    for c in range(DC):
                        ins = pe.matmul(ps_o[:, u % 2, :], yT[:, u % 2, c, :], wp[:, c, :], start=(c == 0),
                                        stop=(c == DC - 1))
                    ins.then_inc(s["o"], 1)
            for t in range(RT):
                pe.wait_ge(s["n"], t + 1)
                pe.wait_ge(s["tT"], RT)
                later(pe, s["xr"], t - 1)
                for c in range(DC):
                    ins = pe.transpose(ps_t[:, t % 2, c, :], y[:, t, c * P:(c + 1) * P], ident[:])
                ins.then_inc(s["xt"], 1)

        @block.scalar
        def _(act):
            act.preload_act_table(ACT.Sqrt)
            for t in range(RT):
                act.wait_ge(s["t"], t + 1)
                later(act, s["o"], t - 1)
                act.activation(yT[:, t % 2, :, :], ps_t[:, t % 2, :, :], ACT.Copy).then_inc(s["tT"], 1)
            act.wait_ge(s["var"], 1)
            act.activation(tmp[:], var[:], ACT.Sqrt).then_inc(s["sqrt"], 1)
            for t in range(RT + 1):
                if t < RT:
                    act.wait_ge(s["xt"], t + 1)
                    act.activation(xh[:, :, t * P:(t + 1) * P], ps_t[:, t % 2, :, :], ACT.Copy).then_inc(s["xh"], 1)
                if t >= 1:
                    u = t - 1
                    act.wait_ge(s["xr"], u + 1)
                    act.activation(xl[:, :, u * P:(u + 1) * P], rest[:, u % 2, :, :], ACT.Copy, scale=1.0 / LOW)\
                       .then_inc(s["xl"], 1)

        @block.vector
        def _(dve):
            c = Chain(dve, s["chain"])

            def weigh(i):
                dve.wait_ge(s["raw"], 16 * (i + 1))
                dve.tensor_reduce(mass[:, i:i + 1], raw[:], X, ALU.add, apply_absolute_value=True)\
                   .then_inc(s["mass"], 1)

            def ternary(i):
                dve.wait_ge(s["total"], i + 1)
                c.link(dve.tensor_scalar(thr[:, 0, i:i + 1], total[:, i:i + 1], 0.5 / (D * FFN), 0.5e-8, ALU.mult, ALU.add))
                c.link(dve.tensor_scalar(thr[:, 1, i:i + 1], thr[:, 0, i:i + 1], -1.0, None, ALU.mult))
                hi, lo = (t1, t2, t3)[i][:, 0, :], (t1, t2, t3)[i][:, 1, :]
                c.link(dve.tensor_scalar(lo, raw[:], thr[:, 1, i:i + 1], None, ALU.is_lt))
                c.link(dve.scalar_tensor_tensor(hi, raw[:], thr[:, 0, i:i + 1], lo, ALU.is_gt, ALU.subtract))
                dve.tensor_scalar(lo, hi, LOW, None, ALU.mult).then_inc(s["tern"], 1)

            weigh(0)
            dve.wait_ge(s["in"], 48)
            dve.wait_ge(s["x"], 16)
            for t in range(RT):
                if t in (3, 7, 11):
                    ternary(t // 4)
                if t in (5, 9):
                    weigh(t // 4)
                dve.wait_ge(s["o"], t + 1)
                c.link(dve.tensor_tensor(y[:, t, :], y[:, t, :], ps_o[:, t % 2, :], ALU.add))
                dve.tensor_tensor(y[:, t, :], y[:, t, :], bp[:], ALU.add).then_inc(s["y"], 1)
                dve.wait_ge(s["y"], t + 1)
                ins = dve.bn_stats(stats[:, t, :], y[:, t, :])
            c.link(ins)
            layer_norm_rows(dve, c, y, stats, mv, mean, rstd, var, tmp, s["var"], s["sqrt"], 1)
            for t in range(RT):
                dve.tensor_scalar(y[:, t, :], y[:, t, :], mean[:, t:t + 1], rstd[:, t:t + 1], ALU.subtract, ALU.mult)\
                   .then_inc(s["n"], 1)
            for t in range(RT):
                dve.wait_ge(s["xh"], t + 1)
                later(dve, s["xl"], t - 1)
                dve.tensor_tensor(rest[:, t % 2, :, :], ps_t[:, t % 2, :, :], xh[:, :, t * P:(t + 1) * P], ALU.subtract)\
                   .then_inc(s["xr"], 1)


def feed_forward(nc, y, t1, t2, t3, xh, xl, out):
    CT = 2
    CR = CT * P
    NC = RT // CT
    with ExitStack() as ctx:
        def sb(name, shape, dt=F32):
            return ctx.enter_context(nc.sbuf_tensor("p6_" + name, shape, dt))

        def pb(name, shape, dt=F32):
            return ctx.enter_context(nc.psum_tensor("p6_" + name, shape, dt))

        def sem(name):
            return ctx.enter_context(nc.semaphore("p6_" + name))

        sig, hid, rest = sb("sig", [P, 2, CR]), sb("hid", [P, 2, CR]), sb("rest", [P, 2, CR])
        hh, hl = sb("hh", [P, 2, MC, CR], FP16), sb("hl", [P, 2, MC, CR], FP16)
        stats, mv = sb("stats", [P, RT * 6]), sb("mv", [P, RT, 2])
        mean, rstd, var, tmp = (sb(n, [P, RT]) for n in ("mean", "rstd", "var", "tmp"))
        ps_1, ps_2, ps_o = pb("ps_1", [P, 2, 512]), pb("ps_2", [P, 2, 512]), pb("ps_o", [P, 2, D])
        s = {n: sem("s_" + n) for n in "u sig hid hh rest hl o y var sqrt n out chain".split()}
        yf = y[:].rearrange("p t d -> p (t d)")

        def chunks(eng, chunk):
            chunk(0, 0)
            with eng.Fori(0, (NC - 1) // 2) as k:
                for half in range(2):
                    chunk(2 * k + 1 + half, 1 - half)
            chunk(NC, 1)

        def is_first(c):
            return isinstance(c, int) and c == 0

        def is_over(c):
            return isinstance(c, int) and c == NC

        block = ctx.enter_context(nc.Block())

        @block.tensor
        def _(pe):
            def up(c, m):
                n = MC * c + m
                later(pe, s["hid"], n - 1)
                for ps, w in ((ps_1, t1), (ps_2, t2)):
                    for q in range(2 * DC):
                        part, k = q // DC, q % DC
                        ins = pe.matmul(ps[:, m_par[0], 0:CR], w[:, part, k * FFN + m * P:k * FFN + (m + 1) * P],
                                        (xh, xl)[part][:, k, ds(c * CR, CR)], start=(q == 0), stop=(q == 2 * DC - 1))
                ins.then_inc(s["u"], 1)
                m_par[0] = 1 - m_par[0]

            def down(c, half):
                pe.wait_ge(s["hl"], MC * (c + 1))
                for u in range(CT):
                    pe.wait_ge(s["y"], CT * c + u + 1)
                    for m in range(MC):
                        for part in range(2):
                            ins = pe.matmul(ps_o[:, u, :], (hh, hl)[part][:, half, m, u * P:(u + 1) * P],
                                            t3[:, part, m * D:(m + 1) * D], start=(m + part == 0),
                                            stop=(m + part == MC))
                    ins.then_inc(s["o"], 1)

            m_par = [0]

            def chunk(c, half):
                m_par[0] = half
                if is_over(c):
                    down(c - 1, 1 - half)
                    return
                for m in range(MC):
                    up(c, m)
                    if m == 2 and not is_first(c):
                        down(c - 1, 1 - half)
            chunks(pe, chunk)

        @block.scalar
        def _(act):
            act.preload_act_table(ACT.Sigmoid)

            def chunk(c, half):
                if is_over(c):
                    for m in range(2):
                        tail(c, half, m)
                    return
                for m in range(MC):
                    n, par = MC * c + m, (m + half) % 2
                    act.wait_ge(s["u"], n + 1)
                    later(act, s["hid"], n - 1)
                    act.activation(sig[:, par, :], ps_1[:, par, 0:CR], ACT.Sigmoid).then_inc(s["sig"], 1)
                    tail(c, half, m)

            def tail(c, half, m):
                n, par = MC * c + m, (m + half) % 2
                if not (is_first(c) and m < 1) and not (is_over(c) and m >= 1):
                    at, hf = (m - 1, half) if m >= 1 else (MC - 1, 1 - half)
                    act.wait_ge(s["hid"], n)
                    act.activation(hh[:, hf, at, :], hid[:, 1 - par, :], ACT.Copy).then_inc(s["hh"], 1)
                if not (is_first(c) and m < 2):
                    at, hf = (m - 2, half) if m >= 2 else (MC - 2 + m, 1 - half)
                    act.wait_ge(s["rest"], n - 1)
                    act.activation(hl[:, hf, at, :], rest[:, par, :], ACT.Copy, scale=1.0 / LOW).then_inc(s["hl"], 1)

            chunks(act, chunk)
            act.wait_ge(s["var"], 1)
            act.activation(tmp[:], var[:], ACT.Sqrt).then_inc(s["sqrt"], 1)

        @block.vector
        def _(dve):
            def hidden(c, half, m):
                n, par = MC * c + m, (m + half) % 2
                dve.wait_ge(s["sig"], n + 1)
                later(dve, s["rest"], n - 1)
                later(dve, s["hh"], n - 1)
                dve.tensor_tensor(hid[:, par, :], ps_2[:, par, 0:CR], sig[:, par, :], ALU.mult).then_inc(s["hid"], 1)

            def left(c, half, m):
                n, par = MC * c + m, (m + half) % 2
                at, hf = (m - 1, half) if m >= 1 else (MC - 1, 1 - half)
                dve.wait_ge(s["hh"], n)
                later(dve, s["hl"], n - 2)
                dve.tensor_tensor(rest[:, 1 - par, :], hid[:, 1 - par, :], hh[:, hf, at, :], ALU.subtract)\
                   .then_inc(s["rest"], 1)

            def rows(c, u):
                t = CT * c + u
                dve.wait_ge(s["o"], t + 1)
                dve.tensor_tensor(yf[:, ds(t * D, D)], yf[:, ds(t * D, D)], ps_o[:, u, :], ALU.add).then_inc(s["y"], 1)
                dve.wait_ge(s["y"], CT + t + 1)
                dve.bn_stats(stats[:, ds(t * 6, 6)], yf[:, ds(t * D, D)]).then_inc(s["n"], 1)

            def chunk(c, half):
                if is_over(c):
                    left(c, half, 0)
                    for u in range(CT):
                        rows(c - 1, u)
                    return
                for m in range(MC):
                    hidden(c, half, m)
                    if not (is_first(c) and m == 0):
                        left(c, half, m)
                    if m in (5, 7) and not is_first(c):
                        rows(c - 1, (m - 5) // 2)

            dve.sem_inc(s["y"], CT)
            chunks(dve, chunk)
            dve.wait_ge(s["n"], RT)
            ch = Chain(dve, s["chain"])
            layer_norm_rows(dve, ch, y, stats[:].rearrange("p (t n) -> p t n", n=6), mv, mean, rstd, var, tmp,
                            s["var"], s["sqrt"], 1)
            for t in range(RT):
                dve.tensor_scalar(y[:, t, :], y[:, t, :], mean[:, t:t + 1], rstd[:, t:t + 1], ALU.subtract, ALU.mult)\
                   .then_inc(s["n"], 1)

        @block.sync
        def _(sp):
            for t in range(RT):
                sp.wait_ge(s["n"], RT + t + 1)
                sp.dma_start(out[t * P:(t + 1) * P, :], y[:, t, :]).then_inc(s["out"], 16)
            sp.wait_ge(s["out"], 16 * RT)


def decoder(nc, a, out):
    x1_dram = nc.dram_tensor("x1_rows", (ROWS, D), F32, kind="Internal").ap()
    qT_dram = nc.dram_tensor("q_ints_T", (D, ROWS), BF16, kind="Internal").ap()
    kT_dram = nc.dram_tensor("k_parts_T", (3, D, KEYS), BF16, kind="Internal").ap()
    v_dram = nc.dram_tensor("v_rows", (KEYS, D), F32, kind="Internal").ap()
    vi_dram = nc.dram_tensor("v_ints", (H, KT, NKT * HD), BF16, kind="Internal").ap()
    with ExitStack() as ctx:
        def sb(name, shape, dt=F32):
            return ctx.enter_context(nc.sbuf_tensor(name, shape, dt))

        sq, svr = sb("q_scales", [P, H, RT]), sb("v_scales", [P, D])
        with nc.sbuf_tensor("aoT", [SK, ROWS], F32) as aoT:
            sparse_attention(nc, a, aoT)
            project_queries(nc, a, aoT, sq, x1_dram, qT_dram)
        project_keys(nc, a, svr, kT_dram, v_dram, vi_dram)
        xo = sb("xo", [P, RT, D])
        cross_attention(nc, a, sq, svr, xo, qT_dram, kT_dram, vi_dram)
        y = sb("y", [P, RT, D])
        t1, t2, t3 = (sb(n, [P, 2, DC * FFN], BF16) for n in ("t1", "t2", "t3"))
        xh, xl = sb("xh", [P, DC, ROWS], FP16), sb("xl", [P, DC, ROWS], FP16)
        output_projection(nc, a, xo, y, t1, t2, t3, xh, xl, x1_dram)
        feed_forward(nc, y, t1, t2, t3, xh, xl, out)


def kernel(**inputs):
    import numpy as _np
    import ml_dtypes as _ml
    import concourse.bacc as _bacc
    from concourse.bass_utils import run_bass_kernel_spmd as _run

    bf = _ml.bfloat16

    def lay(x):
        return _np.ascontiguousarray(x)

    i = {k: _np.asarray(v) for k, v in inputs.items()}
    at = _np.arange(S)
    arrays = {
        "x": lay(i["x"]), "ctxT": lay(i["ctx_2048"].reshape(KEYS, D).T),
        "W1T": lay(i["L0_attn_W1"].T), "WqkvT": lay(i["L0_attn_Wqkv"].T), "W2T": lay(i["L0_attn_W2"].T),
        "W3": lay(i["L0_attn_W3"]), "WoutT": lay(i["L0_attn_Wout"].T),
        "gamma": lay(i["L0_attn_gamma"].reshape(DC, P).T), "beta": lay(i["L0_attn_beta"].reshape(DC, P).T),
        "b1": lay(i["L0_attn_b1"]), "b2": lay(i["L0_attn_b2"]), "b3": lay(i["L0_attn_b3"]),
        "bqkv": lay(i["L0_attn_bqkv"]), "bout": lay(i["L0_attn_bout"]),
        "Wq": lay(i["L0_xattn_Wq"]), "bq": lay(i["L0_xattn_bq"]), "Wkv": lay(i["L0_xattn_Wkv"]),
        "bkv": lay(i["L0_xattn_bkv"]), "Wp": lay(i["L0_xattn_Wp"]), "bp": lay(i["L0_xattn_bp"]),
        "w1T": lay(i["L0_ffn_w1"].T), "w2T": lay(i["L0_ffn_w2"].T), "w3T": lay(i["L0_ffn_w3"].T),
        "ident": _np.eye(P, dtype=_np.float32), "identb": _np.eye(P).astype(bf),
        "tri": (at[:, None] <= at[None]).astype(bf), "offdiag": (1 - _np.eye(S)).astype(_np.float32),
        "rank": lay(_np.broadcast_to(_np.arange(1, TOP + 1)[None, :, None], (S, TOP, S)).astype(bf)),
    }
    nc = _bacc.Bacc("TRN2", target_bir_lowering=False, num_devices=1)
    a = {k: nc.dram_tensor("in_" + k, v.shape, mybir.dt.from_np(v.dtype), kind="ExternalInput").ap()
         for k, v in arrays.items()}
    out = nc.dram_tensor("out_rows", (ROWS, D), F32, kind="ExternalOutput").ap()
    decoder(nc, a, out)
    r = _run(nc, [{"in_" + k: v for k, v in arrays.items()}], core_ids=[0])
    return r.results[0]["out_rows"].reshape(B, S, D)
```

```python
from contextlib import ExitStack

import numpy as np

import concourse.bass as bass
from concourse import mybir

ALU = mybir.AluOpType
ACT = mybir.ActivationFunctionType
F32 = mybir.dt.float32
BF16 = mybir.dt.bfloat16
FP16 = mybir.dt.float16
U16 = mybir.dt.uint16
X = mybir.AxisListType.X
ds = bass.ds

B, S, D = 16, 112, 512
ROWS = B * S
P = 128
RT = ROWS // P
DC = D // P
F1, F2 = 128, 64
SH, SD = 32, 2
SK = SH * SD
TOP = max(1, int(S * 0.1))
GI = 8
NG = S // GI
EPS = 1e-5
FLOOR = -3.0e38
CTX = 375
KEYS = B * CTX
H, HD = 16, 32
KT = 125
NKT = KEYS // KT
NEXP = 3
MAGIC = 1.5 * 2.0 ** 23
FFN = 1408
MC = FFN // P


class Chain:

    def __init__(self, eng, sem, base=0):
        self.eng, self.sem, self.base, self.n = eng, sem, base, 0

    def link(self, ins, carrier=None):
        self.n += 1
        ins.then_inc(self.sem, 1)
        self.eng.wait_ge(self.sem, self.base + self.n)
        if carrier is not None:
            self.eng.memset(carrier, 0.0)


def rstd_newton(dve, chain, rstd, var, tmp):
    chain.link(dve.tensor_tensor(tmp, var, rstd, ALU.mult))
    chain.link(dve.tensor_tensor(tmp, tmp, rstd, ALU.mult))
    chain.link(dve.tensor_scalar(tmp, tmp, -0.5, 1.5, ALU.mult, ALU.add))
    chain.link(dve.tensor_tensor(rstd, rstd, tmp, ALU.mult))


def sparse_attention(nc, a, aoT, ident, identb, ahead):
    POSTL = 18
    PREPL = 5
    RING = NG // 2
    QUAD = 32
    HALF = S // 2
    with ExitStack() as ctx:
        def sb(name, shape, dt=F32):
            return ctx.enter_context(nc.sbuf_tensor("p1_" + name, shape, dt))

        def pb(name, shape, dt=F32):
            return ctx.enter_context(nc.psum_tensor("p1_" + name, shape, dt))

        def sem(name):
            return ctx.enter_context(nc.semaphore("p1_" + name))

        xa = sb("xa", [S, B * D])
        w1 = sb("w1", [P, DC, F1])
        wqkv = sb("wqkv", [P, DC, 3 * SK])
        gamma, beta = sb("gamma", [P, DC]), sb("beta", [P, DC])
        b1, b2 = sb("b1", [P, 1]), sb("b2", [P, 1])
        w2 = sb("w2", [F1, F2])
        w3 = sb("w3", [P, 2])
        w3g = sb("w3g", [P, RING * (QUAD + 2)])
        b3 = sb("b3", [2 * QUAD, 1])
        bqkv = sb("bqkv", [S, 3 * SK])
        tri = sb("tri", [S, S], BF16)
        offdiag = sb("offdiag", [S, S])
        rank = sb("rank", [S, TOP, S], BF16)

        stats = sb("stats", [S, B * 6])
        mv = sb("mv", [S, B, 2])
        var, mean, rstd, tmp = (sb(n, [S, B]) for n in ("var", "mean", "rstd", "tmp"))
        xn = sb("xn", [S, D])
        xnT = sb("xnT", [P, DC, S])
        hb = sb("hb", [F1, 2, S])
        hn = sb("hn", [F1, 2, S])
        qkv = sb("qkv", [S, 2, 3 * SK])
        kvp = sb("kvp", [S, 2, 3, 2 * SK], BF16)
        kvr = sb("kvr", [S, 2, 2 * SK])
        pair = sb("pair", [F1, RING, GI * S])
        u = sb("u", [P, RING, GI // 2 * S])
        sims = sb("sims", [2 * QUAD, GI // 2 * S])
        simr = sb("simr", [S, S])
        sim = sb("sim", [S, S])
        best = sb("best", [S, 16])
        wait_col = sb("wait_col", [S, 1])
        rest, rest2 = sb("rest", [S, S]), sb("rest2", [S, S])
        mask = sb("mask", [S, S], BF16)
        maskT = sb("maskT", [S, S], BF16)
        rankT = sb("rankT", [S, S], BF16)
        onehot = sb("onehot", [S, TOP, S], BF16)
        prod = sb("prod", [S, TOP, SK])
        sc, ex = sb("sc", [S, TOP, SH]), sb("ex", [S, TOP, SH])
        mx, den, rden = sb("mx", [S, SH]), sb("den", [S, SH]), sb("rden", [S, SH])
        ao = sb("ao", [S, P])

        ps_xT = pb("ps_xT", [P, DC, P])
        ps_hq = pb("ps_hq", [P, 512])
        ps_u = pb("ps_u", [P, 2, 512])
        ps_sim = pb("ps_sim", [2 * QUAD, 512])
        ps_one = pb("ps_one", [P, 512])
        ps_g = pb("ps_g", [S, 2, 512])
        NH1 = 512 // SK

        XQ = 4
        s_in, s_x = sem("s_in"), [sem(f"s_x{q}") for q in range(XQ)]
        s_w3z, s_w3g, s_aoz, s_stat, s_sqrt = sem("s_w3z"), sem("s_w3g"), sem("s_aoz"), sem("s_stat"), sem("s_sqrt")
        s_pc, s_prep, s_start = sem("s_pc"), sem("s_prep"), sem("s_start")
        s_xn, s_xT, s_xnT, s_hq, s_hb, s_hn, s_kvp = (sem(n) for n in ("s_xn", "s_xT", "s_xnT", "s_hq", "s_hb", "s_hn", "s_kvp"))
        s_pairv, s_paira, s_mm1, s_u, s_mm2 = (sem(n) for n in ("s_pairv", "s_paira", "s_mm1", "s_u", "s_mm2"))
        s_sims, s_sim, s_mask, s_mT, s_mTs, s_cum, s_oh = (sem(n) for n in ("s_sims", "s_sim", "s_mask", "s_mT", "s_mTs", "s_cum", "s_oh"))
        s_gk, s_sc, s_ex, s_gv, s_ao, s_aoT, s_aoTs = (sem(n) for n in ("s_gk", "s_sc", "s_ex", "s_gv", "s_ao", "s_aoT", "s_aoTs"))

        AHEAD = 2
        V, T, A = (4, 6, 8, 11, 13, 0, 13), (3, 5, 7, 10, 13, 0, 2), (9, 13, 1, 5)
        DV = 5
        loads = [
            (w1[:], a["W1T"].rearrange("(c p) f -> p c f", p=P)),
            (wqkv[:], a["WqkvT"].rearrange("(c p) f -> p c f", p=P)),
            (gamma[:], a["gamma"]),
            (beta[:], a["beta"]),
            (b1[:], a["b1"].rearrange("(p a) -> p a", a=1)),
            (b2[0:F2], a["b2"].rearrange("(p a) -> p a", a=1)),
            (b2[F2:P], a["b2"].rearrange("(p a) -> p a", a=1)),
            (w2[:], a["W2T"]),
            (b3[:], a["b3"].rearrange("(p a) -> p a", a=1).broadcast_to([2 * QUAD, 1])),
            (bqkv[:], a["bqkv"].rearrange("(p a) -> p a", p=1).broadcast_to([S, 3 * SK])),
            (ident[:], a["ident"]), (identb[:], a["identb"]), (tri[:], a["tri"]),
            (offdiag[:], a["offdiag"]), (rank[:], a["rank"]),
        ]
        LOADED = 16 * len(loads) + 32

        def schedule(eng_steps, pair_step, last=None):
            for g in range(NG):
                pair_step(g)
                for at, step in eng_steps:
                    if at == g:
                        step()
            if last:
                last()

        def row(g, r):
            return HALF * (g % 2) + GI * (g // 2) + r

        def batches(eng, run):
            run(0, 0, post=False, prep=True)
            with eng.Fori(0, (B - 2) // 2) as k:
                for half in range(2):
                    run(2 * k + 1 + half, (1 + half) % 2, post=True, prep=True)
            run(B - 1, (B - 1) % 2, post=True, prep=False)
            run(B, 0, post=True, prep=False)

        block = ctx.enter_context(nc.Block())

        @block.sync
        def _(sp):
            for q in range(XQ):
                at = slice(q * B // XQ, (q + 1) * B // XQ)
                sp.dma_start(xa[:].rearrange("s (b d) -> s b d", b=B)[:, at, :],
                             a["x"].rearrange("b s d -> s b d")[:, at, :]).then_inc(s_x[q], 16)
            for out, src in loads:
                sp.dma_start(out, src).then_inc(s_in, 16)
            sp.wait_ge(s_w3z, 2)
            w3col = a["W3"].rearrange("a f -> f a")
            sp.dma_start(w3[0:F2, 0:1], w3col).then_inc(s_in, 16)
            sp.dma_start(w3[F2:P, 1:2], w3col).then_inc(s_in, 16)
            for inputs in ahead:
                fetch(sp, inputs)
            with sp.Fori(0, B) as b:
                sp.wait_ge(s_sims, b + 1)
                sp.wait_ge(s_mask, b + 1)
                for odd in range(2):
                    sp.dma_start(simr[odd * HALF:(odd + 1) * HALF, :],
                                 sims[odd * QUAD:odd * QUAD + NG, :].rearrange("m (r j) -> m r j", j=S)).then_inc(s_sim, 16)
            sp.wait_ge(s_sim, 32 * B)

        @block.vector
        def _(dve):
            dve.memset(w3[:], 0.0).then_inc(s_w3z, 1)
            dve.memset(w3g[:], 0.0).then_inc(s_w3z, 1)
            dve.sem_inc(s_mask, 1)
            dve.memset(ao[:], 0.0).then_inc(s_aoz, 1)
            dve.wait_ge(s_aoz, 1)
            start = Chain(dve, s_start)
            for b in range(B):
                if b % (B // XQ) == 0:
                    dve.wait_ge(s_x[b * XQ // B], 16)
                dve.bn_stats(stats[:, 6 * b:6 * b + 6], xa[:, b * D:(b + 1) * D]).then_inc(s_stat, 1)
            dve.wait_ge(s_in, LOADED)
            dve.wait_ge(s_w3z, 2)
            dve.tensor_copy(w3g[:].rearrange("p (m c) -> p m c", m=RING)[:, :, 0:2],
                            w3[:].unsqueeze(1).broadcast_to([P, RING, 2])).then_inc(s_w3g, 1)
            dve.wait_ge(s_stat, B)
            for b in range(B):
                dve.bn_aggr(mv[:, b, :], stats[:, 6 * b:6 * b + 6]).then_inc(s_stat, 1)
            dve.wait_ge(s_stat, 2 * B)
            start.link(dve.tensor_scalar(var[:], mv[:, :, 1], EPS, None, ALU.add))
            start.link(dve.tensor_copy(mean[:], mv[:, :, 0]))
            dve.wait_ge(s_sqrt, 1)
            start.link(dve.reciprocal(rstd[:], tmp[:]))
            rstd_newton(dve, start, rstd[:], var[:], tmp[:])

            def normalise(b):
                if not isinstance(b, int) or b > 0:
                    dve.wait_ge(s_xT, b)
                dve.tensor_scalar(xn[:], xa[:, ds(b * D, D)], mean[:, ds(b, 1)], rstd[:, ds(b, 1)],
                                  ALU.subtract, ALU.mult).then_inc(s_xn, 1)

            def project(b, par):
                dve.wait_ge(s_hb, b + 1)
                c = Chain(dve, s_prep, PREPL * b)
                dve.tensor_scalar(hn[:, par, :], ps_hq[:, 0:S], -1.0, None, ALU.mult).then_inc(s_hn, 1)
                c.link(dve.tensor_tensor(qkv[:, par, :], ps_hq[0:S, 256:256 + 3 * SK], bqkv[:], ALU.add))
                kv = qkv[:, par, SK:3 * SK]
                c.link(dve.tensor_copy(kvp[:, par, 0, :], kv))
                c.link(dve.tensor_tensor(kvr[:, 0, :], kv, kvp[:, par, 0, :], ALU.subtract))
                c.link(dve.tensor_copy(kvp[:, par, 1, :], kvr[:, 0, :]))
                c.link(dve.tensor_tensor(kvr[:, 1, :], kvr[:, 0, :], kvp[:, par, 1, :], ALU.subtract))
                dve.tensor_copy(kvp[:, par, 2, :], kvr[:, 1, :]).then_inc(s_kvp, 1)

            def topk(b, c):
                dve.wait_ge(s_sim, 32 * (b + 1))
                c.link(dve.tensor_tensor(sim[:], simr[:], offdiag[:], ALU.mult), wait_col[:])
                c.link(dve.max(best[:, 0:8], sim[:]), wait_col[:])
                c.link(dve.match_replace(rest[:], best[:, 0:8], sim[:], FLOOR), wait_col[:])
                c.link(dve.max(best[:, 8:16], rest[:]))
                c.link(dve.memset(best[:, TOP:16], FLOOR), wait_col[:])
                c.link(dve.match_replace(rest2[:], best[:, 8:16], rest[:], FLOOR))
                dve.tensor_scalar(mask[:], rest2[:], FLOOR, None, ALU.is_equal).then_inc(s_mask, 1)

            def onehots(b, c):
                dve.wait_ge(s_cum, b + 1)
                c.link(dve.tensor_tensor(rankT[:], ps_one[0:S, 0:S], maskT[:], ALU.mult))
                dve.tensor_tensor(onehot[:], rankT[:].unsqueeze(1).broadcast_to([S, TOP, S]), rank[:],
                                  ALU.is_equal).then_inc(s_oh, 1)

            def scores(b, par, c):
                dve.wait_ge(s_gk, b + 1)
                q = qkv[:, par, 0:SK].unsqueeze(1)
                for lo, hi in ((0, NH1), (NH1, TOP)):
                    c.link(dve.tensor_tensor(prod[:, lo:hi, :],
                                             ps_g[:, lo // NH1, 0:(hi - lo) * SK].rearrange("s (t e) -> s t e", e=SK),
                                             q.broadcast_to([S, hi - lo, SK]), ALU.mult))
                pr = prod[:].rearrange("s t (h e) -> s (t h) e", e=SD)
                c.link(dve.tensor_tensor(sc[:].rearrange("s t h -> s (t h)"), pr[:, :, 0], pr[:, :, 1], ALU.add))
                c.link(dve.tensor_reduce(mx[:], sc[:].rearrange("s t h -> s h t"), X, ALU.max))
                dve.tensor_tensor(sc[:], sc[:], mx[:].unsqueeze(1).broadcast_to([S, TOP, SH]),
                                  ALU.subtract).then_inc(s_sc, 1)

            def mix(b, c):
                dve.wait_ge(s_ex, b + 1)
                c.link(dve.tensor_reduce(den[:], ex[:].rearrange("s t h -> s h t"), X, ALU.add))
                c.link(dve.reciprocal(rden[:], den[:]))
                dve.wait_ge(s_gv, b + 1)
                for e in range(SD):
                    for lo, hi in ((0, NH1), (NH1, TOP)):
                        g = ps_g[:, lo // NH1, 0:(hi - lo) * SK].rearrange("s (t h e) -> s t h e", h=SH, e=SD)
                        o = prod[:].rearrange("s t (h e) -> s t h e", e=SD)
                        c.link(dve.tensor_tensor(o[:, lo:hi, :, e], g[:, :, :, e], ex[:, lo:hi, :], ALU.mult))
                c.link(dve.tensor_reduce(ao[:, 0:SK], prod[:].rearrange("s t k -> s k t"), X, ALU.add))
                dve.tensor_tensor(ao[:, 0:SK].rearrange("s (h e) -> s h e", e=SD), ao[:, 0:SK].rearrange("s (h e) -> s h e", e=SD),
                                  rden[:].unsqueeze(2).broadcast_to([S, SH, SD]), ALU.mult).then_inc(s_ao, 1)

            def run(b, par, post, prep):
                steps = []
                if post:
                    c = Chain(dve, s_pc, (b - 1) * POSTL)
                    steps += [(V[0], lambda: topk(b - 1, c)), (V[1], lambda: mask_copy(b - 1)),
                              (V[2], lambda: onehots(b - 1, c)), (V[3], lambda: scores(b - 1, 1 - par, c)),
                              (V[4], lambda: mix(b - 1, c))]
                if prep:
                    steps += [(V[5], lambda: normalise(b + 1)), (V[6], lambda: project(b + 1, 1 - par))]
                if isinstance(b, int) and b == B:
                    for _, step in steps:
                        step()
                else:
                    def pairs(g):
                        if g == 0:
                            dve.wait_ge(s_hn, b + 1)
                            dve.wait_ge(s_hb, b + 1)
                        later(dve, s_mm1, NG * b + g - RING + 1)
                        for r in range(DV):
                            i = row(g, r)
                            ins = dve.tensor_scalar(pair[:, g % RING, r * S:(r + 1) * S], hn[:, par, :],
                                                    hb[:, par, i:i + 1], 0.0, ALU.add, ALU.max)
                        ins.then_inc(s_pairv, 1)
                    schedule(steps, pairs)
                if post:
                    assert c.n <= POSTL, c.n
                    used.append(c.n)

            def mask_copy(b):
                dve.wait_ge(s_mT, b + 1)
                dve.tensor_copy(maskT[:], ps_one[:].bitcast(BF16)[0:S, 0:S]).then_inc(s_mTs, 1)

            used = []
            normalise(0)
            project(0, 0)
            batches(dve, run)
            assert set(used) == {POSTL}, used

        @block.scalar
        def _(act):
            act.wait_ge(s_start, 2)
            act.activation(tmp[:], var[:], ACT.Sqrt).then_inc(s_sqrt, 1)
            act.preload_act_table(ACT.Exp)

            def evac_x(b):
                act.wait_ge(s_xT, b + 1)
                for c in range(DC):
                    act.activation(xnT[:, c, :], ps_xT[:, c, 0:S], ACT.Identity, bias=beta[:, c:c + 1],
                                   scale=gamma[:, c:c + 1]).then_inc(s_xnT, 1)

            def evac_h(b, par):
                act.wait_ge(s_hq, b + 1)
                act.activation(hb[:, par, :], ps_hq[:, 0:S], ACT.Identity, bias=b1[:, 0:1]).then_inc(s_hb, 1)

            def evac_sim(b):
                act.wait_ge(s_mm2, NG * (b + 1))
                act.wait_ge(s_mask, b + 1)
                act.activation(sims[:], ps_sim[:, 0:GI // 2 * S], ACT.Identity, bias=b3[:, 0:1]).then_inc(s_sims, 1)

            def exps(b):
                act.wait_ge(s_sc, b + 1)
                act.activation(ex[:], sc[:], ACT.Exp, scale=float(1.0 / np.sqrt(SD))).then_inc(s_ex, 1)

            def evac_ao(b):
                act.wait_ge(s_aoT, b + 1)
                act.activation(aoT[:, ds(b * S, S)], ps_one[0:SK, 0:S], ACT.Copy).then_inc(s_aoTs, 1)

            def run(b, par, post, prep):
                steps = []
                if post:
                    steps += [(0, lambda: evac_sim(b - 1)), (A[0], lambda: exps(b - 1)), (A[1], lambda: evac_ao(b - 1))]
                if prep:
                    steps += [(A[2], lambda: evac_x(b + 1)), (A[3], lambda: evac_h(b + 1, 1 - par))]
                if isinstance(b, int) and b == B:
                    for _, step in steps:
                        step()
                    return

                def pairs(g):
                    later(act, s_mm1, NG * b + g - RING + 1)
                    for r in range(DV, GI):
                        i = row(g, r)
                        ins = act.activation(pair[:, g % RING, r * S:(r + 1) * S], hn[:, par, :], ACT.Relu,
                                             bias=hb[:, par, i:i + 1])
                    ins.then_inc(s_paira, 1)

                def relus(g):
                    if g == 0:
                        act.wait_ge(s_hn, b + 1)
                        act.wait_ge(s_hb, b + 1)
                        for ahead in range(AHEAD):
                            pairs(ahead)
                    if g + AHEAD < NG:
                        pairs(g + AHEAD)
                    act.wait_ge(s_mm1, NG * b + g + 1)
                    later(act, s_mm2, NG * b + g - RING + 1)
                    act.activation(u[:, g % RING, :], ps_u[:, g % 2, 0:GI // 2 * S], ACT.Relu,
                                   bias=b2[:, 0:1]).then_inc(s_u, 1)
                schedule(steps, relus)

            act.sem_inc(s_aoTs, 1)
            act.wait_ge(s_in, LOADED)
            evac_x(0)
            evac_h(0, 0)
            batches(act, run)

        @block.tensor
        def _(pe):
            pe.wait_ge(s_in, LOADED)
            pe.wait_ge(s_w3g, 1)

            def transpose_x(b):
                pe.wait_ge(s_xn, b + 1)
                if not isinstance(b, int) or b > 0:
                    pe.wait_ge(s_xnT, DC * b)
                for c in range(DC):
                    ins = pe.transpose(ps_xT[:, c, 0:S], xn[:, c * P:(c + 1) * P], ident[0:S, 0:S])
                ins.then_inc(s_xT, 1)

            def hqkv(b):
                pe.wait_ge(s_xnT, DC * (b + 1))
                if not isinstance(b, int) or b > 0:
                    pe.wait_ge(s_kvp, b)
                for c in range(DC):
                    pe.matmul(ps_hq[:, 0:S], w1[:, c, :], xnT[:, c, :], start=(c == 0), stop=(c == DC - 1))
                for c in range(DC):
                    ins = pe.matmul(ps_hq[0:S, 256:256 + 3 * SK], xnT[:, c, :], wqkv[:, c, :],
                                    start=(c == 0), stop=(c == DC - 1))
                ins.then_inc(s_hq, 1)

            def layer3(b, g):
                if g % 2 == 0:
                    pe.wait_ge(s_u, NG * b + g + 2)
                if g == 0 and (not isinstance(b, int) or b > 0):
                    pe.wait_ge(s_sims, b)
                at = g % 2 * QUAD
                pe.matmul(ps_sim[at:at + QUAD, 0:GI // 2 * S], w3g[:, g // 2 * QUAD:(g // 2 + 1) * QUAD],
                          u[:, g % RING, :], start=(g < 2), stop=(g >= NG - 2)).then_inc(s_mm2, 1)

            def mask_back(b):
                pe.wait_ge(s_mask, b + 2)
                pe.wait_ge(s_aoTs, b + 1)
                pe.transpose(ps_one[:].bitcast(BF16)[0:S, 0:S], mask[:], identb[0:S, 0:S]).then_inc(s_mT, 1)

            def count(b):
                pe.wait_ge(s_mTs, b + 1)
                pe.matmul(ps_one[0:S, 0:S], tri[:], maskT[:], start=True, stop=True).then_inc(s_cum, 1)

            def gather(par, lo, signal):
                for t in range(TOP):
                    out = ps_g[:, t // NH1, (t % NH1) * SK:(t % NH1 + 1) * SK]
                    for part in range(3):
                        ins = pe.matmul(out, onehot[:, t, :], kvp[:, par, part, lo:lo + SK],
                                        start=(part == 0), stop=(part == 2))
                ins.then_inc(signal, 1)

            def gather_k(b, par):
                pe.wait_ge(s_oh, b + 1)
                pe.wait_ge(s_kvp, b + 1)
                gather(par, 0, s_gk)

            def gather_v(b, par):
                pe.wait_ge(s_sc, b + 1)
                gather(par, SK, s_gv)

            def ao_back(b):
                pe.wait_ge(s_ao, b + 1)
                pe.transpose(ps_one[:, 0:S], ao[:], ident[0:S, 0:S]).then_inc(s_aoT, 1)

            def run(b, par, post, prep):
                steps = []
                if post:
                    steps += [(T[0], lambda: mask_back(b - 1)), (T[1], lambda: count(b - 1)),
                              (T[2], lambda: gather_k(b - 1, 1 - par)), (T[3], lambda: gather_v(b - 1, 1 - par)),
                              (T[4], lambda: ao_back(b - 1))]
                if prep:
                    steps += [(T[5], lambda: transpose_x(b + 1)), (T[6], lambda: hqkv(b + 1))]
                if isinstance(b, int) and b == B:
                    for _, step in steps:
                        step()
                    return

                def layer2(g):
                    pe.wait_ge(s_pairv, NG * b + g + 1)
                    pe.wait_ge(s_paira, NG * b + g + 1)
                    if g >= 2 or not isinstance(b, int) or b > 0:
                        pe.wait_ge(s_u, NG * b + g - 1)
                    half = GI // 2 * S
                    for side in range(2):
                        ins = pe.matmul(ps_u[side * F2:(side + 1) * F2, g % 2, 0:half], w2[:],
                                        pair[:, g % RING, side * half:(side + 1) * half], start=True, stop=True)
                    ins.then_inc(s_mm1, 1)
                    if g >= 2 and g % 2 == 0:
                        layer3_pair(g - 2)

                def layer3_pair(g):
                    layer3(b, g)
                    layer3(b, g + 1)
                schedule(steps, layer2, last=lambda: layer3_pair(NG - 2))

            transpose_x(0)
            hqkv(0)
            batches(pe, run)


def fetch(sp, inputs):
    for out, src in inputs[1]:
        sp.dma_start(out, src).then_inc(inputs[2], 16)


def row_of(vector, rows):
    return vector.rearrange("(o n) -> o n", o=1).broadcast_to([rows, vector.shape[0]])


def later(eng, sem, value):
    if not isinstance(value, int) or value > 0:
        eng.wait_ge(sem, value)


def layer_norm_rows(dve, c, y, stats, mv, mean, rstd, var, tmp, s_var, s_sqrt, sqrts):
    for t in range(RT):
        ins = dve.bn_aggr(mv[:, t, :], stats[:, t, :])
    c.link(ins)
    c.link(dve.tensor_copy(mean[:], mv[:, :, 0]))
    dve.tensor_scalar(var[:], mv[:, :, 1], EPS, None, ALU.add).then_inc(s_var, 1)
    dve.wait_ge(s_var, sqrts)
    dve.wait_ge(s_sqrt, sqrts)
    c.link(dve.reciprocal(rstd[:], tmp[:]))
    rstd_newton(dve, c, rstd[:], var[:], tmp[:])


def query_inputs(nc, ctx, a):
    y, wout, wq, bout, bq = (ctx.enter_context(nc.sbuf_tensor("p2_" + n, shape, F32)) for n, shape in (
        ("y", [P, RT, D]), ("wout", [SK, D]), ("wq", [P, DC, D]), ("bout", [P, D]), ("bq", [P, D])))
    return (y, wout, wq, bout, bq), [
        (y[:], a["x"].rearrange("b s d -> (b s) d").rearrange("(t p) d -> p t d", p=P)),
        (wout[:], a["WoutT"]), (wq[:], a["Wq"].rearrange("(c p) n -> p c n", p=P)),
        (bout[:], row_of(a["bout"], P)), (bq[:], row_of(a["bq"], P)),
    ], ctx.enter_context(nc.semaphore("p2_s_in"))


def project_queries(nc, a, inputs, aoT, sq, ident, identb, x1_dram, qT_dram):
    with ExitStack() as ctx:
        def sb(name, shape, dt=F32):
            return ctx.enter_context(nc.sbuf_tensor("p2_" + name, shape, dt))

        def pb(name, shape, dt=F32):
            return ctx.enter_context(nc.psum_tensor("p2_" + name, shape, dt))

        def sem(name):
            return ctx.enter_context(nc.semaphore("p2_" + name))

        (y, wout, wq, bout, bq), loads, s_in = inputs
        stats, mv = sb("stats", [P, RT, 6]), sb("mv", [P, RT, 2])
        mean, rstd, var, tmp = (sb(n, [P, RT]) for n in ("mean", "rstd", "var", "tmp"))
        yT = sb("yT", [P, 2, DC, P])
        qf, qn = sb("qf", [P, H, HD]), sb("qn", [P, H, HD])
        qi = sb("qi", [P, 2, D], BF16)
        am, rq = sb("am", [P, H]), sb("rq", [P, H])
        qT = sb("qT", [P, DC, ROWS], BF16)
        ps_o, ps_t, ps_q = pb("ps_o", [P, 2, D]), pb("ps_t", [P, 2, DC, P]), pb("ps_q", [P, 2, D])
        ps_i = pb("ps_i", [P, 2, 2 * D], BF16)
        names = "o y var sqrt x1 c t tT q qi i qT st"
        s = {n: sem("s_" + n) for n in names.split()}
        LOADED = 16 * len(loads)
        SCALE = float(1.0 / np.sqrt(HD))
        block = ctx.enter_context(nc.Block())

        @block.sync
        def _(sp):
            sp.wait_ge(s["x1"], RT)
            sp.dma_start(x1_dram.rearrange("(t p) d -> p t d", p=P), y[:]).then_inc(s["st"], 16)
            for lo, hi in ((0, RT - 3), (RT - 3, RT)):
                sp.wait_ge(s["qT"], hi)
                sp.dma_start(qT_dram.rearrange("(c p) n -> p c n", p=P)[:, :, lo * P:hi * P], qT[:, :, lo * P:hi * P])\
                    .then_inc(s["st"], 16)
            sp.wait_ge(s["st"], 48)

        @block.tensor
        def _(pe):
            pe.wait_ge(s_in, LOADED)
            for t in range(RT):
                later(pe, s["y"], t - 1)
                pe.matmul(ps_o[:, t % 2, :], aoT[:, t * P:(t + 1) * P], wout[:], start=True, stop=True)\
                    .then_inc(s["o"], 1)

            def queries(t):
                pe.wait_ge(s["tT"], t + 1)
                later(pe, s["q"], t - 1)
                for c in range(DC):
                    ins = pe.matmul(ps_q[:, t % 2, :], yT[:, t % 2, c, :], wq[:, c, :], start=(c == 0),
                                    stop=(c == DC - 1))
                ins.then_inc(s["c"], 1)

            def turn(t):
                pe.wait_ge(s["qi"], t + 1)
                later(pe, s["qT"], t - 1)
                for c in range(DC):
                    ins = pe.transpose(ps_i[:, t % 2, c * P:(c + 1) * P], qi[:, t % 2, c * P:(c + 1) * P], identb[:])
                ins.then_inc(s["i"], 1)

            for t in range(RT + 2):
                if t < RT:
                    pe.wait_ge(s["x1"], t + 1)
                    later(pe, s["tT"], t - 1)
                    for c in range(DC):
                        ins = pe.transpose(ps_t[:, t % 2, c, :], y[:, t, c * P:(c + 1) * P], ident[:])
                    ins.then_inc(s["t"], 1)
                if 1 <= t <= RT:
                    queries(t - 1)
                if t >= 2:
                    turn(t - 2)

        @block.scalar
        def _(act):
            act.wait_ge(s["var"], 1)
            act.activation(tmp[:], var[:], ACT.Sqrt).then_inc(s["sqrt"], 1)
            for t in range(RT + 2):
                if t < RT:
                    act.wait_ge(s["t"], t + 1)
                    later(act, s["c"], t - 1)
                    act.activation(yT[:, t % 2, :, :], ps_t[:, t % 2, :, :], ACT.Copy).then_inc(s["tT"], 1)
                if t >= 2:
                    u = t - 2
                    act.wait_ge(s["i"], u + 1)
                    act.activation(qT[:, :, u * P:(u + 1) * P], ps_i[:, u % 2, 0:D].rearrange("p (c n) -> p c n", c=DC),
                                   ACT.Copy).then_inc(s["qT"], 1)

        @block.vector
        def _(dve):
            c = Chain(dve, sem("s_chain"))
            dve.wait_ge(s_in, LOADED)
            for t in range(RT):
                dve.wait_ge(s["o"], t + 1)
                c.link(dve.scalar_tensor_tensor(y[:, t, :], y[:, t, :], 2.0, ps_o[:, t % 2, :], ALU.mult, ALU.add))
                dve.tensor_tensor(y[:, t, :], y[:, t, :], bout[:], ALU.add).then_inc(s["y"], 1)
                dve.wait_ge(s["y"], t + 1)
                ins = dve.bn_stats(stats[:, t, :], y[:, t, :])
            c.link(ins)
            layer_norm_rows(dve, c, y, stats, mv, mean, rstd, var, tmp, s["var"], s["sqrt"], 1)
            for t in range(RT):
                dve.tensor_scalar(y[:, t, :], y[:, t, :], mean[:, t:t + 1], rstd[:, t:t + 1], ALU.subtract, ALU.mult)\
                   .then_inc(s["x1"], 1)
            for t in range(RT):
                dve.wait_ge(s["c"], t + 1)
                dve.tensor_tensor(qf[:].rearrange("p h d -> p (h d)"), ps_q[:, t % 2, :], bq[:], ALU.add)\
                   .then_inc(s["q"], 1)
                dve.wait_ge(s["q"], t + 1)
                c.link(dve.tensor_reduce(am[:], qf[:], X, ALU.max, apply_absolute_value=True))
                c.link(dve.tensor_scalar(sq[:, :, t], am[:], SCALE / 127.0, 1e-8, ALU.mult, ALU.max))
                c.link(dve.reciprocal(rq[:], sq[:, :, t]))
                c.link(dve.tensor_scalar(rq[:], rq[:], SCALE, None, ALU.mult))
                c.link(dve.tensor_tensor(qn[:], qf[:], rq[:].unsqueeze(2).broadcast_to([P, H, HD]), ALU.mult))
                later(dve, s["i"], t - 1)
                dve.tensor_scalar(qi[:, t % 2, :], qn[:].rearrange("p h d -> p (h d)"), MAGIC, MAGIC,
                                  ALU.add, ALU.subtract).then_inc(s["qi"], 1)


CH = 2 * KT


def context_source(a, ch):
    return a["ctxT"].rearrange("(c p) n -> p c n", p=P)[:, :, ds(ch * CH, CH)]


def context_inputs(nc, ctx, a):
    ctxT = ctx.enter_context(nc.sbuf_tensor("p3_ctxT", [P, 2, DC, CH], F32))
    return [(ctxT, [(ctxT[:, half], context_source(a, half))], ctx.enter_context(nc.semaphore(f"p3_s_ctx{half}")))
            for half in range(2)]


def key_inputs(nc, ctx, a):
    wkv, bk, bv = (ctx.enter_context(nc.sbuf_tensor("p3_" + n, shape, F32)) for n, shape in (
        ("wkv", [P, DC, 2 * D]), ("bk", [KT, D]), ("bv", [KT, D])))
    return (wkv, bk, bv), [
        (wkv[:], a["Wkv"].rearrange("(c p) n -> p c n", p=P)),
        (bk[:], row_of(a["bkv"][0:D], KT)), (bv[:], row_of(a["bkv"][D:2 * D], KT)),
    ], ctx.enter_context(nc.semaphore("p3_s_in"))


def project_keys(nc, a, inputs, context, svr, rv, identb, kT_dram, v_dram):
    with ExitStack() as ctx:
        def sb(name, shape, dt=F32):
            return ctx.enter_context(nc.sbuf_tensor("p3_" + name, shape, dt))

        def pb(name, shape, dt=F32):
            return ctx.enter_context(nc.psum_tensor("p3_" + name, shape, dt))

        def sem(name):
            return ctx.enter_context(nc.semaphore("p3_" + name))

        R = 4
        (wkv, bk, bv), loads, s_in = inputs
        ctxT, s_ctx = context[0][0], [of_half[2] for of_half in context]
        kf, kn = sb("kf", [KT, H, HD]), sb("kn", [KT, H, HD])
        am, sk, rk = sb("am", [KT, H]), sb("sk", [KT, H]), sb("rk", [KT, H])
        kd = sb("kd", [KT, R, D])
        kd2 = sb("kd2", [KT, 2, D])
        kd3 = sb("kd3", [KT, 2, D])
        part = sb("part", [KT, R, 3, D], BF16)
        kTs = sb("kTs", [P, 2, DC * 3, CH], BF16)
        vf = sb("vf", [KT, R, D])
        vmax, vall = sb("vmax", [P, D]), sb("vall", [P, D])
        ps_k, ps_v = pb("ps_k", [KT, 2, D]), pb("ps_v", [KT, 2, D])
        ps_T = pb("ps_T", [P, 2, 16, P], BF16)
        s = {n: sem("s_" + n) for n in ("k v kf vf kd h m l r2 r3 T ev kst chain vmax vmz vr chain2").split()}
        s_kst = [s["kst"], sem("s_kst1")]
        s_vst = [sem(f"s_vst_{i}") for i in range(R)]
        LOADED = 16 * len(loads)
        NCH = NKT // 2
        LAG = 3

        def steps(eng, step):
            for j in range(R):
                step(j, j)
            with eng.Fori(1, NKT // R) as k:
                for r in range(R):
                    step(k * R + r, r)
            for j in range(NKT, NKT + LAG):
                step(j, j % R)

        def has(j, lag):
            return not (isinstance(j, int) and (j < lag or j - lag >= NKT))

        block = ctx.enter_context(nc.Block())

        @block.sync
        def _(sp):
            def load(ch, half):
                sp.wait_ge(s["v"], 2 * (ch - 1))
                sp.dma_start(ctxT[:, half, :, :], context_source(a, ch)).then_inc(s_ctx[half], 16)

            def store_v(ch, half):
                for sub in range(2):
                    sp.wait_ge(s["vf"], 2 * ch + sub + 1)
                    sp.dma_start(v_dram[ds((2 * ch + sub) * KT, KT), :], vf[:, 2 * half + sub, :])\
                      .then_inc(s_vst[2 * half + sub], 16)

            def store_k(ch, half):
                sp.wait_ge(s["ev"], 2 * (ch + 1))
                dst = kT_dram.rearrange("a (c p) n -> p c a n", p=P)
                for c in range(DC):
                    sp.dma_start(dst[:, c, :, ds(ch * CH, CH)], kTs[:, half, c * 3:(c + 1) * 3, :])\
                      .then_inc(s_kst[half], 16)

            for ch in range(2):
                load(ch + 2, ch)
                store_v(ch, ch)
            with sp.Fori(1, NCH // 2 - 1) as k:
                for half in range(2):
                    load(2 * k + 2 + half, half)
                    store_v(2 * k + half, half)
                    store_k(2 * k - 2 + half, half)
            for half in range(2):
                store_v(NCH - 2 + half, half)
                store_k(NCH - 4 + half, half)
            for half in range(2):
                store_k(NCH - 2 + half, half)
            for half in range(2):
                sp.wait_ge(s_kst[half], 16 * DC * NCH // 2)
            for r in range(R):
                sp.wait_ge(s_vst[r], 16 * NKT // R)

        @block.gpsimd
        def _(pool):
            def step(j, r):
                if has(j, 0):
                    pool.wait_ge(s["h"], j + 1)
                    later(pool, s["m"], j - 1)
                    later(pool, s["r3"], j - 1)
                    pool.tensor_tensor(kd2[:, r % 2, :], kd[:, r, :], part[:, r, 0, :], ALU.subtract)\
                        .then_inc(s["r2"], 1)
                if has(j, 1):
                    pool.wait_ge(s["m"], j)
                    pool.wait_ge(s["r2"], j)
                    later(pool, s["l"], j - 2)
                    pool.tensor_tensor(kd3[:, (r - 1) % 2, :], kd2[:, (r - 1) % 2, :], part[:, (r - 1) % R, 1, :],
                                       ALU.subtract).then_inc(s["r3"], 1)
            steps(pool, step)
            pool.wait_ge(s["vmax"], NKT)
            pool.partition_all_reduce(vall[:], vmax[:], P, bass.bass_isa.ReduceOp.max).then_inc(s["vr"], 1)

        @block.tensor
        def _(pe):
            pe.wait_ge(s_in, LOADED)

            def step(j, r):
                if has(j, 0):
                    half, sub = r // 2, r % 2
                    pe.wait_ge(s_ctx[half], 16 * (j // R + 1) if isinstance(j, int) else 16 * (quotient[0] + 1))
                    for w, (ps, done, used) in enumerate(((ps_k, s["k"], s["kf"]), (ps_v, s["v"], s["vf"]))):
                        later(pe, used, j - 1)
                        for c in range(DC):
                            ins = pe.matmul(ps[:, r % 2, :], ctxT[:, half, c, sub * KT:(sub + 1) * KT],
                                            wkv[:, c, w * D:(w + 1) * D], start=(c == 0), stop=(c == DC - 1))
                        ins.then_inc(done, 1)
                if has(j, LAG):
                    o = (r - LAG) % R
                    pe.wait_ge(s["l"], j - LAG + 1)
                    later(pe, s["ev"], j - LAG)
                    for c in range(DC):
                        for n in range(3):
                            ins = pe.transpose(ps_T[:, (c * 3 + n) // 8, (c * 3 + n) % 8, 0:KT],
                                               part[:, o, n, c * P:(c + 1) * P], identb[0:KT, 0:KT])
                    ins.then_inc(s["T"], 1)

            quotient = [0]
            for j in range(R):
                step(j, j)
            with pe.Fori(1, NKT // R) as k:
                quotient[0] = k
                for r in range(R):
                    step(k * R + r, r)
            for j in range(NKT, NKT + LAG):
                step(j, j % R)

        @block.scalar
        def _(act):
            def step(j, r):
                if has(j, 0):
                    act.wait_ge(s["kd"], j + 1)
                    later(act, s["T"], j - R + 1)
                    act.activation(part[:, r, 0, :], kd[:, r, :], ACT.Copy).then_inc(s["h"], 1)
                if has(j, 1):
                    act.wait_ge(s["r2"], j)
                    act.activation(part[:, (r - 1) % R, 1, :], kd2[:, (r - 1) % 2, :], ACT.Copy).then_inc(s["m"], 1)
                if has(j, 2):
                    act.wait_ge(s["r3"], j - 1)
                    act.activation(part[:, (r - 2) % R, 2, :], kd3[:, (r - 2) % 2, :], ACT.Copy).then_inc(s["l"], 1)
                if has(j, LAG):
                    o = (r - LAG) % R
                    act.wait_ge(s["T"], j - LAG + 1)
                    if not (isinstance(j, int) and j - LAG < R):
                        if isinstance(j, int):
                            act.wait_ge(s_kst[o // 2], 16 * DC * ((j - LAG) // R))
                        else:
                            act.wait_ge(s_kst[o // 2], 16 * DC * (quotient[0] if r >= LAG else quotient[0] - 1))
                    for b, n in ((0, 8), (1, 4)):
                        ins = act.activation(kTs[:, o // 2, b * 8:b * 8 + n, (o % 2) * KT:(o % 2 + 1) * KT],
                                             ps_T[:, b, 0:n, 0:KT], ACT.Copy)
                    ins.then_inc(s["ev"], 1)

            quotient = [0]
            for j in range(R):
                step(j, j)
            for j in range(R, 2 * R):
                step(j, j % R)
            with act.Fori(2, NKT // R) as k:
                quotient[0] = k
                for r in range(R):
                    step(k * R + r, r)
            for j in range(NKT, NKT + LAG):
                step(j, j % R)

        @block.vector
        def _(dve):
            dve.memset(vmax[:], 0.0).then_inc(s["vmz"], 1)
            dve.wait_ge(s_in, LOADED)
            dve.wait_ge(s["vmz"], 1)
            LINKS = 6

            def tile(j, r):
                c = Chain(dve, s["chain"], LINKS * j)
                dve.wait_ge(s["k"], j + 1)
                dve.tensor_tensor(kf[:].rearrange("p h d -> p (h d)"), ps_k[:, r % 2, :], bk[:], ALU.add)\
                   .then_inc(s["kf"], 1)
                dve.wait_ge(s["v"], j + 1)
                if quotient[0] is not None:
                    dve.wait_ge(s_vst[r], 16 * quotient[0])
                dve.tensor_tensor(vf[:, r, :], ps_v[:, r % 2, :], bv[:], ALU.add).then_inc(s["vf"], 1)
                dve.wait_ge(s["kf"], j + 1)
                c.link(dve.tensor_reduce(am[:], kf[:], X, ALU.max, apply_absolute_value=True))
                c.link(dve.tensor_scalar(sk[:], am[:], 1.0 / 127.0, 1e-8, ALU.mult, ALU.max))
                c.link(dve.reciprocal(rk[:], sk[:]))
                c.link(dve.tensor_tensor(kn[:], kf[:], rk[:].unsqueeze(2).broadcast_to([KT, H, HD]), ALU.mult))
                dve.wait_ge(s["vf"], j + 1)
                c.link(dve.scalar_tensor_tensor(vmax[0:KT, :], vf[:, r, :], -1.0, vmax[0:KT, :], ALU.mult, ALU.max))
                c.link(dve.tensor_scalar(kn[:], kn[:], MAGIC, MAGIC, ALU.add, ALU.subtract))
                dve.tensor_tensor(vmax[0:KT, :], vmax[0:KT, :], vf[:, r, :], ALU.max).then_inc(s["vmax"], 1)
                if quotient[0] is not None:
                    dve.wait_ge(s["r2"], j - R + 1)
                dve.tensor_tensor(kd[:, r, :].rearrange("p (h d) -> p h d", h=H), kn[:],
                                  sk[:].unsqueeze(2).broadcast_to([KT, H, HD]), ALU.mult).then_inc(s["kd"], 1)

            quotient = [None]
            for j in range(R):
                tile(j, j)
            with dve.Fori(1, NKT // R) as k:
                quotient[0] = k
                for r in range(R):
                    tile(k * R + r, r)
            c = Chain(dve, s["chain2"])
            dve.wait_ge(s["vr"], 1)
            c.link(dve.tensor_scalar(svr[:], vall[:], 1.0 / 127.0, 1e-8, ALU.mult, ALU.max))
            c.link(dve.reciprocal(rv[:], svr[:]))


def cross_attention(nc, sq, svr, rv, xo, identb, ahead, qT_dram, kT_dram, v_dram):
    with ExitStack() as ctx:
        def sb(name, shape, dt=F32):
            return ctx.enter_context(nc.sbuf_tensor("p4_" + name, shape, dt))

        def pb(name, shape, dt=F32):
            return ctx.enter_context(nc.psum_tensor("p4_" + name, shape, dt))

        def sem(name):
            return ctx.enter_context(nc.semaphore("p4_" + name))

        SG = 6
        GW = KEYS // SG
        MW = GW // 2
        NB = 6
        TB = NKT // NB
        EP = KEYS // NEXP
        LN255 = float(np.log(255.0))

        kT = sb("kT", [3 * HD, 2, KEYS], BF16)
        qs = sb("qs", [3 * HD, 2, ROWS], BF16)
        vh = sb("vh", [KT, 2, NKT * HD], BF16)
        vf = sb("vf", [KT, NKT * HD])
        nsq = sb("nsq", [P, H * RT])
        sc = sb("sc", [P, 2, KEYS])
        e = sb("e", [P, KEYS], U16)
        et = sb("et", [KT, NB, TB * P], BF16)
        top = sb("top", [P, 2, SG])
        mx, bias = sb("mx", [P, 2]), sb("bias", [P, 2])
        sums = sb("sums", [P, 2, RT * NEXP])
        den, rden = sb("den", [P, RT]), sb("rden", [P, RT])
        on = sb("on", [P, RT, HD])
        ps_s = pb("ps_s", [P, 2, 2, 512])
        ps_t = pb("ps_t", [KT, 2, TB * P], BF16)
        ps_o = pb("ps_o", [P, 2, 512])
        s = {n: sem("s_" + n) for n in "nsq qk copy top bias exp T evd eva pv chain norm vf vn vr free round".split()}
        s_kq = [sem("s_kq0"), sem("s_kq1")]
        ND = 6
        NORM = (0, 1, 3, 4)
        FEW = 4
        TURN, COPY = 3, 4

        block = ctx.enter_context(nc.Block())

        @block.sync
        def _(sp):
            def load(h, hp):
                if not isinstance(h, int) or h >= 2:
                    sp.wait_ge(s["qk"], SG * RT * (h - 1))
                for part in range(3):
                    sp.dma_start(kT[part * HD:(part + 1) * HD, hp, :], kT_dram[part, ds(h * HD, HD), :])\
                      .then_inc(s_kq[hp], 16)
                    sp.dma_start(qs[part * HD:(part + 1) * HD, hp, :], qT_dram[ds(h * HD, HD), :])\
                      .then_inc(s_kq[hp], 16)
                later(sp, s["vr"], h)
                sp.sem_inc(s["free"], 1)
                sp.dma_start(vf[:].rearrange("p (j d) -> p j d", d=HD), vd[:, :, ds(h * HD, HD)]).then_inc(s["vf"], 16)
            vd = v_dram.rearrange("(j p) d -> p j d", p=KT)
            load(0, 0)
            load(1, 1)
            fetch(sp, ahead)
            with sp.Fori(1, H // 2) as k:
                for hp in range(2):
                    load(2 * k + hp, hp)

        def is_first(n):
            return isinstance(n, int) and n == 0

        def heads(eng, first, step, finish):
            first()
            step(0, 0, 0, 0, 0)

            def head(k, hp, last):
                base = RT * (2 * k + hp)
                with eng.Fori(0, (RT - 2) // FEW) as m:
                    for i in range(FEW):
                        step(base + FEW * m + 1 + i, FEW * m + 1 + i, (1 + i) % 2, hp, k)
                step(base + RT - 1, RT - 1, 1, hp, k, last=last)
                if not last:
                    step(base + RT, 0, 0, 1 - hp, k + hp)
            head(0, 0, False)
            with eng.Fori(0, H // 2 - 1) as k:
                head(k, 1, False)
                head(k + 1, 0, False)
            head(H // 2 - 1, 1, True)
            finish()

        @block.gpsimd
        def _(pool):
            def values(h, hp):
                pool.wait_ge(s["vf"], 16 * (h + 1))
                pool.tensor_tensor(vf[:].rearrange("p (j d) -> p j d", d=HD), vf[:].rearrange("p (j d) -> p j d", d=HD),
                                   rv[0:KT, ds(h * HD, HD)].unsqueeze(1).broadcast_to([KT, NKT, HD]), ALU.mult)\
                    .then_inc(s["vn"], 1)
                pool.wait_ge(s["vn"], h + 1)
                if not isinstance(h, int) or h >= 2:
                    pool.wait_ge(s["pv"], NB + NB * RT * (h - 1))
                pool.sem_inc(s["round"], 1)
                pool.tensor_scalar(vh[:, hp, :], vf[:], MAGIC, MAGIC, ALU.add, ALU.subtract).then_inc(s["vr"], 1)
            values(0, 0)
            values(1, 1)
            with pool.Fori(1, H // 2) as k:
                for hp in range(2):
                    values(2 * k + hp, hp)

        @block.tensor
        def _(pe):
            pe.sem_inc(s["pv"], NB)

            def products(n, g, t, hp, k):
                if g == 0 and isinstance(t, int) and t == 0:
                    pe.wait_ge(s_kq[hp], 16 * ND * (k + 1))
                later(pe, s["copy"], SG * n + g - 1)
                for b in range(2):
                    ins = pe.matmul(ps_s[:, g % 2, b, 0:MW], qs[:, hp, ds(t * P, P)],
                                    kT[:, hp, g * GW + b * MW:g * GW + (b + 1) * MW], start=True, stop=True)
                ins.then_inc(s["qk"], 1)

            def turn(n, i):
                pe.wait_ge(s["exp"], NEXP * n + i * NEXP // NB + 1)
                later(pe, s["evd"] if i % 2 == 0 else s["eva"], NB // 2 * n + i // 2)
                for j in range(TB):
                    at = (i * TB + j) * KT
                    ins = pe.transpose(ps_t[:, i % 2, j * P:(j + 1) * P], e[:, at:at + KT].bitcast(BF16), identb[:])
                ins.then_inc(s["T"], 1)

            def attend(n, i, t, hp, k):
                pe.wait_ge(s["evd"] if i % 2 == 0 else s["eva"], NB // 2 * n + i // 2 + 1)
                for j in range(TB):
                    ins = pe.matmul(ps_o[:, hp, ds(t * HD, HD)], et[:, i, j * P:(j + 1) * P],
                                    vh[:, hp, (i * TB + j) * HD:(i * TB + j + 1) * HD],
                                    start=(i == 0 and j == 0), stop=(i == NB - 1 and j == TB - 1))
                ins.then_inc(s["pv"], 1)

            def step(n, t, par, hp, k, last=False):
                if isinstance(t, int) and t == RT - 1:
                    nxt = (0, 1 - hp, k + hp)
                else:
                    nxt = (t + 1, hp, k)
                before = (t - 1, hp, k) if not (isinstance(t, int) and t == 0) else (RT - 1, 1 - hp, k + hp - 1)
                for g in range(SG):
                    if g == SG - 1 and isinstance(t, int) and t == 0:
                        pe.wait_ge(s["vr"], 2 * k + hp + 1)
                        later(pe, s["norm"], 2 * k + hp)
                    if not last:
                        products(n + 1, g, *nxt)
                    if not is_first(n):
                        attend(n - 1, g, *before)
                    if g % 2 == 1:
                        for lag in (TURN + 1, TURN):
                            if g >= lag:
                                turn(n, g - lag)
                            elif not is_first(n):
                                turn(n - 1, g - lag + NB)
            def first():
                for g in range(SG):
                    products(0, g, 0, 0, 0)

            def finish():
                n = H * RT - 1
                for g in range(NB):
                    attend(n, g, RT - 1, 1, H // 2 - 1)
                    if g % 2 == 1 and g <= TURN:
                        turn(n, g - TURN - 1 + NB)
                        if g < TURN:
                            turn(n, g - TURN + NB)
            heads(pe, first, step, finish)

        @block.scalar
        def _(act):
            act.preload_act_table(ACT.Exp)
            act.wait_ge(s["nsq"], 1)

            def evac(n, i):
                act.wait_ge(s["T"], NB * n + i + 1)
                act.wait_ge(s["pv"], NB * n + i + 1)
                act.activation(et[:, i, :], ps_t[:, i % 2, :].bitcast(U16), ACT.Copy).then_inc(s["eva"], 1)

            def step(n, t, par, hp, k, last=False):
                for part in range(NEXP):
                    if part == 0:
                        act.wait_ge(s["bias"], n + 1)
                        act.sem_inc(s["free"], 1)
                    act.activation(e[:, part * EP:(part + 1) * EP], sc[:, par, part * EP:(part + 1) * EP], ACT.Exp,
                                   bias=bias[:, par:par + 1], scale=sq[:].rearrange("p h t -> p (h t)")[:, ds(n, 1)],
                                   accum_out=sums[:, hp, ds(t * NEXP + part, 1)]).then_inc(s["exp"], 1)
                    if part == NEXP - 1:
                        evac(n, 1)
                    elif not is_first(n):
                        evac(n - 1, 2 * part + 3)

            def finish():
                evac(H * RT - 1, 3)
                evac(H * RT - 1, 5)
            heads(act, lambda: None, step, finish)

        @block.vector
        def _(dve):
            dve.tensor_scalar(nsq[:], sq[:].rearrange("p h t -> p (h t)"), -1.0, None, ALU.mult).then_inc(s["nsq"], 1)
            dve.wait_ge(s["nsq"], 1)

            def copies(n, g, par):
                if g == 0:
                    later(dve, s["exp"], NEXP * (n - 1))
                dve.wait_ge(s["qk"], SG * n + g + 1)
                dve.tensor_scalar(sc[:, par, g * GW:(g + 1) * GW].rearrange("p (b n) -> p b n", b=2),
                                  ps_s[:, g % 2, :, 0:MW], 1.0, None, ALU.mult, ALU.max,
                                  accum_out=top[:, par, g:g + 1]).then_inc(s["copy"], 1)

            def maxima(n, par):
                dve.wait_ge(s["copy"], SG * (n + 1))
                dve.tensor_reduce(mx[:, par:par + 1], top[:, par, :], X, ALU.max).then_inc(s["top"], 1)

            def biases(n, par):
                dve.wait_ge(s["top"], n + 1)
                dve.tensor_scalar(bias[:, par:par + 1], mx[:, par:par + 1], nsq[:, ds(n, 1)], LN255,
                                  ALU.mult, ALU.add).then_inc(s["bias"], 1)

            def evac(n, i):
                dve.wait_ge(s["T"], NB * n + i + 1)
                dve.wait_ge(s["pv"], NB * n + i + 1)
                dve.tensor_copy(et[:, i, :], ps_t[:, i % 2, :].bitcast(U16)).then_inc(s["evd"], 1)

            def normalise(h, hp, part):
                if part == 0:
                    dve.wait_ge(s["pv"], NB + NB * RT * (h + 1))
                else:
                    dve.wait_ge(s["chain"], 3 * h + part)
                if part == 0:
                    dve.tensor_reduce(den[:], sums[:, hp, :].rearrange("p (t n) -> p t n", n=NEXP), X, ALU.add)\
                       .then_inc(s["chain"], 1)
                elif part == 1:
                    dve.reciprocal(rden[:], den[:]).then_inc(s["chain"], 1)
                elif part == 2:
                    dve.tensor_tensor(on[:], ps_o[:, hp, 0:RT * HD].rearrange("p (t d) -> p t d", d=HD),
                                      rden[:].unsqueeze(2).broadcast_to([P, RT, HD]), ALU.mult).then_inc(s["chain"], 1)
                else:
                    dve.tensor_tensor(xo[:, :, ds(h * HD, HD)], on[:],
                                      svr[:, ds(h * HD, HD)].unsqueeze(1).broadcast_to([P, RT, HD]), ALU.mult)\
                       .then_inc(s["norm"], 1)

            def step(n, t, par, hp, k, last=False):
                for g in range(SG):
                    if g >= COPY and (g - COPY) % 2 == 0:
                        evac(n, g - COPY)
                    if 0 < g < COPY and (g - COPY) % 2 == 0 and not is_first(n):
                        evac(n - 1, g - COPY + NB)
                    if not last:
                        copies(n + 1, g, 1 - par)
                    if isinstance(t, int) and t == RT - 1 and not (isinstance(k, int) and 2 * k + hp == 0) and g in NORM:
                        normalise(2 * k + hp - 1, 1 - hp, NORM.index(g))
                if not last:
                    maxima(n + 1, 1 - par)
                evac(n, NB - COPY)
                if not last:
                    biases(n + 1, 1 - par)

            def first():
                for g in range(SG):
                    copies(0, g, 0)
                maxima(0, 0)
                biases(0, 0)

            def finish():
                evac(H * RT - 1, 4)
                for part in range(4):
                    normalise(H - 1, 1, part)
            dve.memset(den[:], 1.0).then_inc(s["norm"], 1)
            heads(dve, first, step, finish)


LOW = 2.0 ** -12


def weight_sources(a):
    return [a[n].rearrange("(c p) n -> p c n", p=P) for n in ("w1T", "w2T", "w3T")]


def projection_inputs(nc, ctx, a):
    wp, bp, raw0, raw1 = (ctx.enter_context(nc.sbuf_tensor("p5_" + n, shape, F32)) for n, shape in (
        ("wp", [P, DC, D]), ("bp", [P, D]), ("raw0", [P, DC * FFN]), ("raw1", [P, DC * FFN])))
    return (wp, bp, raw0, raw1), [
        (wp[:], a["Wp"].rearrange("(c p) n -> p c n", p=P)), (bp[:], row_of(a["bp"], P)),
        (raw0[:].rearrange("p (c n) -> p c n", c=DC), weight_sources(a)[0]),
        (raw1[:].rearrange("p (c n) -> p c n", c=DC), weight_sources(a)[1]),
    ], ctx.enter_context(nc.semaphore("p5_s_in"))


def output_projection(nc, a, inputs, ident, xo, y, t1, t2, t3, xh, xl, x1_dram):
    with ExitStack() as ctx:
        def sb(name, shape, dt=F32):
            return ctx.enter_context(nc.sbuf_tensor("p5_" + name, shape, dt))

        def pb(name, shape, dt=F32):
            return ctx.enter_context(nc.psum_tensor("p5_" + name, shape, dt))

        def sem(name):
            return ctx.enter_context(nc.semaphore("p5_" + name))

        (wp, bp, raw0, raw1), loads, s_in = inputs
        raw = (raw0, raw1, raw0)
        PC = 4
        PW = DC * FFN // PC
        mass, total, thr = sb("mass", [P, 3 * PC]), sb("total", [P, 3 * PC]), sb("thr", [P, 3, 3])
        stats, mv = sb("stats", [P, RT, 6]), sb("mv", [P, RT, 2])
        mean, rstd, var, tmp = (sb(n, [P, RT]) for n in ("mean", "rstd", "var", "tmp"))
        yT = sb("yT", [P, 2, DC, P])
        rest = sb("rest", [P, 2, DC, P])
        ps_t, ps_o = pb("ps_t", [P, 2, DC, P]), pb("ps_o", [P, 2, D])
        s = {n: sem("s_" + n) for n in "raw x t tT o y var sqrt n xt xh xr xl mass total tern low chain".split()}
        WEIGH, TERNARY, SCALE = (None, 0, 6), (1, 5, 10), (3, 7, 12)

        def pieces(firsts, t):
            return [(i, t - f) for i, f in enumerate(firsts) if f is not None and f <= t < f + PC]

        block = ctx.enter_context(nc.Block())

        @block.sync
        def _(sp):
            sp.dma_start(y[:], x1_dram.rearrange("(t p) d -> p t d", p=P)).then_inc(s["x"], 16)
            sp.wait_ge(s["mass"], PC)
            sp.wait_ge(s["tern"], PC)
            w = weight_sources(a)[2]
            sp.dma_start(raw[2][:].rearrange("p (c n) -> p c n", c=w.shape[1]), w).then_inc(s["raw"], 16)

        @block.gpsimd
        def _(pool):
            for i in range(3):
                pool.wait_ge(s["mass"], PC * (i + 1))
                at = slice(PC * i, PC * (i + 1))
                pool.partition_all_reduce(total[:, at], mass[:, at], P, bass.bass_isa.ReduceOp.add)\
                    .then_inc(s["total"], 1)

        @block.tensor
        def _(pe):
            pe.wait_ge(s_in, 16 * len(loads))
            for t in range(RT + 1):
                if t < RT:
                    later(pe, s["tT"], t - 1)
                    for c in range(DC):
                        ins = pe.transpose(ps_t[:, t % 2, c, :], xo[:, t, c * P:(c + 1) * P], ident[:])
                    ins.then_inc(s["t"], 1)
                if t >= 1:
                    u = t - 1
                    pe.wait_ge(s["tT"], u + 1)
                    later(pe, s["y"], u - 1)
                    for c in range(DC):
                        ins = pe.matmul(ps_o[:, u % 2, :], yT[:, u % 2, c, :], wp[:, c, :], start=(c == 0),
                                        stop=(c == DC - 1))
                    ins.then_inc(s["o"], 1)
            for t in range(RT):
                pe.wait_ge(s["n"], t + 1)
                pe.wait_ge(s["tT"], RT)
                later(pe, s["xr"], t - 1)
                for c in range(DC):
                    ins = pe.transpose(ps_t[:, t % 2, c, :], y[:, t, c * P:(c + 1) * P], ident[:])
                ins.then_inc(s["xt"], 1)

        @block.scalar
        def _(act):
            act.preload_act_table(ACT.Sqrt)

            def weigh(i, piece):
                if piece == 0 and i == 0:
                    act.wait_ge(s_in, 16 * len(loads))
                if piece == 0 and i == 2:
                    act.wait_ge(s["raw"], 16)
                at = slice(PW * piece, PW * (piece + 1))
                act.activation((t1, t2, t3)[i][:, 0, at], raw[i][:, at], ACT.Abs,
                               accum_out=mass[:, PC * i + piece:PC * i + piece + 1]).then_inc(s["mass"], 1)

            def low(i, piece):
                act.wait_ge(s["tern"], PC * i + piece + 1)
                t, at = (t1, t2, t3)[i], slice(PW * piece, PW * (piece + 1))
                act.activation(t[:, 1, at], t[:, 0, at], ACT.Copy, scale=LOW).then_inc(s["low"], 1)

            for piece in range(PC):
                weigh(0, piece)
            for t in range(RT):
                act.wait_ge(s["t"], t + 1)
                later(act, s["o"], t - 1)
                act.activation(yT[:, t % 2, :, :], ps_t[:, t % 2, :, :], ACT.Copy).then_inc(s["tT"], 1)
                for at in pieces(WEIGH, t):
                    weigh(*at)
                for at in pieces(SCALE, t):
                    low(*at)
            act.wait_ge(s["var"], 1)
            act.activation(tmp[:], var[:], ACT.Sqrt).then_inc(s["sqrt"], 1)
            for t in range(RT, RT + PC):
                for at in pieces(SCALE, t):
                    low(*at)
            for t in range(RT + 1):
                if t < RT:
                    act.wait_ge(s["xt"], t + 1)
                    act.activation(xh[:, :, t * P:(t + 1) * P], ps_t[:, t % 2, :, :], ACT.Copy).then_inc(s["xh"], 1)
                if t >= 1:
                    u = t - 1
                    act.wait_ge(s["xr"], u + 1)
                    act.activation(xl[:, :, u * P:(u + 1) * P], rest[:, u % 2, :, :], ACT.Copy, scale=1.0 / LOW)\
                       .then_inc(s["xl"], 1)

        @block.vector
        def _(dve):
            c = Chain(dve, s["chain"])

            def ternary(i, piece):
                if piece == 0:
                    dve.wait_ge(s["total"], i + 1)
                    c.link(dve.tensor_reduce(thr[:, 2, i:i + 1], total[:, PC * i:PC * (i + 1)], X, ALU.add))
                    c.link(dve.tensor_scalar(thr[:, 0, i:i + 1], thr[:, 2, i:i + 1], 0.5 / (D * FFN), 0.5e-8, ALU.mult, ALU.add))
                    c.link(dve.tensor_scalar(thr[:, 1, i:i + 1], thr[:, 0, i:i + 1], -1.0, None, ALU.mult))
                at = slice(PW * piece, PW * (piece + 1))
                hi, lo = (t1, t2, t3)[i][:, 0, at], (t1, t2, t3)[i][:, 1, at]
                c.link(dve.tensor_scalar(lo, raw[i][:, at], thr[:, 1, i:i + 1], None, ALU.is_lt))
                dve.scalar_tensor_tensor(hi, raw[i][:, at], thr[:, 0, i:i + 1], lo, ALU.is_gt, ALU.subtract)\
                   .then_inc(s["tern"], 1)

            dve.wait_ge(s_in, 16 * len(loads))
            dve.wait_ge(s["x"], 16)
            for t in range(RT):
                dve.wait_ge(s["o"], t + 1)
                c.link(dve.tensor_tensor(y[:, t, :], y[:, t, :], ps_o[:, t % 2, :], ALU.add))
                dve.tensor_tensor(y[:, t, :], y[:, t, :], bp[:], ALU.add).then_inc(s["y"], 1)
                dve.wait_ge(s["y"], t + 1)
                ins = dve.bn_stats(stats[:, t, :], y[:, t, :])
                if t == RT - 1:
                    c.link(ins)
                for at in pieces(TERNARY, t):
                    ternary(*at)
            layer_norm_rows(dve, c, y, stats, mv, mean, rstd, var, tmp, s["var"], s["sqrt"], 1)
            for t in range(RT + 2):
                if t < RT:
                    dve.tensor_scalar(y[:, t, :], y[:, t, :], mean[:, t:t + 1], rstd[:, t:t + 1], ALU.subtract, ALU.mult)\
                       .then_inc(s["n"], 1)
                if t >= 2:
                    u = t - 2
                    dve.wait_ge(s["xh"], u + 1)
                    later(dve, s["xl"], u - 1)
                    dve.tensor_tensor(rest[:, u % 2, :, :], ps_t[:, u % 2, :, :], xh[:, :, u * P:(u + 1) * P],
                                      ALU.subtract).then_inc(s["xr"], 1)


def feed_forward(nc, room, y, t1, t2, t3, xh, xl, out):
    CT = 2
    CR = CT * P
    NC = RT // CT
    with ExitStack() as ctx:
        def sb(name, shape, dt=F32):
            return ctx.enter_context(nc.sbuf_tensor("p6_" + name, shape, dt))

        def pb(name, shape, dt=F32):
            return ctx.enter_context(nc.psum_tensor("p6_" + name, shape, dt))

        def sem(name):
            return ctx.enter_context(nc.semaphore("p6_" + name))

        sig, hid, rest = sb("sig", [P, 2, CR]), sb("hid", [P, 2, CR]), sb("rest", [P, 2, CR])
        parts = room[:].bitcast(FP16).rearrange("p (part h m r) -> p part h m r", part=2, h=2, m=MC)
        hh, hl = parts[:, 0], parts[:, 1]
        stats, mv = sb("stats", [P, RT * 6]), sb("mv", [P, RT, 2])
        mean, rstd, var, tmp = (sb(n, [P, RT]) for n in ("mean", "rstd", "var", "tmp"))
        ps_1, ps_2, ps_o = pb("ps_1", [P, 2, 512]), pb("ps_2", [P, 2, 512]), pb("ps_o", [P, 2, D])
        s = {n: sem("s_" + n) for n in "u sig hid hh rest hl o y var sqrt n out chain".split()}
        yf = y[:].rearrange("p t d -> p (t d)")

        def chunks(eng, chunk):
            chunk(0, 0)
            with eng.Fori(0, (NC - 1) // 2) as k:
                for half in range(2):
                    chunk(2 * k + 1 + half, 1 - half)
            chunk(NC, 1)

        def is_first(c):
            return isinstance(c, int) and c == 0

        def is_over(c):
            return isinstance(c, int) and c == NC

        block = ctx.enter_context(nc.Block())

        @block.tensor
        def _(pe):
            def up(c, m):
                n = MC * c + m
                later(pe, s["hid"], n - 1)
                for ps, w in ((ps_1, t1), (ps_2, t2)):
                    for q in range(2 * DC):
                        part, k = q // DC, q % DC
                        ins = pe.matmul(ps[:, m_par[0], 0:CR], w[:, part, k * FFN + m * P:k * FFN + (m + 1) * P],
                                        (xh, xl)[part][:, k, ds(c * CR, CR)], start=(q == 0), stop=(q == 2 * DC - 1))
                ins.then_inc(s["u"], 1)
                m_par[0] = 1 - m_par[0]

            def down(c, half):
                pe.wait_ge(s["hl"], MC * (c + 1))
                for u in range(CT):
                    pe.wait_ge(s["y"], CT * c + u + 1)
                    for m in range(MC):
                        for part in range(2):
                            ins = pe.matmul(ps_o[:, u, :], (hh, hl)[part][:, half, m, u * P:(u + 1) * P],
                                            t3[:, part, m * D:(m + 1) * D], start=(m + part == 0),
                                            stop=(m + part == MC))
                    ins.then_inc(s["o"], 1)

            m_par = [0]

            def chunk(c, half):
                m_par[0] = half
                if is_over(c):
                    down(c - 1, 1 - half)
                    return
                for m in range(MC):
                    up(c, m)
                    if m == 2 and not is_first(c):
                        down(c - 1, 1 - half)
            chunks(pe, chunk)

        @block.scalar
        def _(act):
            act.preload_act_table(ACT.Sigmoid)

            def chunk(c, half):
                if is_over(c):
                    for m in range(2):
                        tail(c, half, m)
                    return
                for m in range(MC):
                    n, par = MC * c + m, (m + half) % 2
                    act.wait_ge(s["u"], n + 1)
                    later(act, s["hid"], n - 1)
                    act.activation(sig[:, par, :], ps_1[:, par, 0:CR], ACT.Sigmoid).then_inc(s["sig"], 1)
                    tail(c, half, m)

            def tail(c, half, m):
                n, par = MC * c + m, (m + half) % 2
                if not (is_first(c) and m < 1) and not (is_over(c) and m >= 1):
                    at, hf = (m - 1, half) if m >= 1 else (MC - 1, 1 - half)
                    act.wait_ge(s["hid"], n)
                    act.activation(hh[:, hf, at, :], hid[:, 1 - par, :], ACT.Copy).then_inc(s["hh"], 1)
                if not (is_first(c) and m < 2):
                    at, hf = (m - 2, half) if m >= 2 else (MC - 2 + m, 1 - half)
                    act.wait_ge(s["rest"], n - 1)
                    act.activation(hl[:, hf, at, :], rest[:, par, :], ACT.Copy, scale=1.0 / LOW).then_inc(s["hl"], 1)

            chunks(act, chunk)
            act.wait_ge(s["var"], 1)
            act.activation(tmp[:], var[:], ACT.Sqrt).then_inc(s["sqrt"], 1)

        @block.vector
        def _(dve):
            def hidden(c, half, m):
                n, par = MC * c + m, (m + half) % 2
                dve.wait_ge(s["sig"], n + 1)
                later(dve, s["rest"], n - 1)
                later(dve, s["hh"], n - 1)
                dve.tensor_tensor(hid[:, par, :], ps_2[:, par, 0:CR], sig[:, par, :], ALU.mult).then_inc(s["hid"], 1)

            def left(c, half, m):
                n, par = MC * c + m, (m + half) % 2
                at, hf = (m - 1, half) if m >= 1 else (MC - 1, 1 - half)
                dve.wait_ge(s["hh"], n)
                later(dve, s["hl"], n - 2)
                dve.tensor_tensor(rest[:, 1 - par, :], hid[:, 1 - par, :], hh[:, hf, at, :], ALU.subtract)\
                   .then_inc(s["rest"], 1)

            def rows(c, u):
                t = CT * c + u
                dve.wait_ge(s["o"], t + 1)
                dve.tensor_tensor(yf[:, ds(t * D, D)], yf[:, ds(t * D, D)], ps_o[:, u, :], ALU.add).then_inc(s["y"], 1)
                dve.wait_ge(s["y"], CT + t + 1)
                dve.bn_stats(stats[:, ds(t * 6, 6)], yf[:, ds(t * D, D)]).then_inc(s["n"], 1)

            def chunk(c, half):
                if is_over(c):
                    left(c, half, 0)
                    for u in range(CT):
                        rows(c - 1, u)
                    return
                for m in range(MC):
                    hidden(c, half, m)
                    if not (is_first(c) and m == 0):
                        left(c, half, m)
                    if m in (5, 7) and not is_first(c):
                        rows(c - 1, (m - 5) // 2)

            dve.sem_inc(s["y"], CT)
            chunks(dve, chunk)
            dve.wait_ge(s["n"], RT)
            ch = Chain(dve, s["chain"])
            layer_norm_rows(dve, ch, y, stats[:].rearrange("p (t n) -> p t n", n=6), mv, mean, rstd, var, tmp,
                            s["var"], s["sqrt"], 1)
            for t in range(RT):
                dve.tensor_scalar(y[:, t, :], y[:, t, :], mean[:, t:t + 1], rstd[:, t:t + 1], ALU.subtract, ALU.mult)\
                   .then_inc(s["n"], 1)

        @block.sync
        def _(sp):
            for t in range(RT):
                sp.wait_ge(s["n"], RT + t + 1)
                sp.dma_start(out[t * P:(t + 1) * P, :], y[:, t, :]).then_inc(s["out"], 16)
            sp.wait_ge(s["out"], 16 * RT)


def decoder(nc, a, out):
    x1_dram = nc.dram_tensor("x1_rows", (ROWS, D), F32, kind="Internal").ap()
    qT_dram = nc.dram_tensor("q_ints_T", (D, ROWS), BF16, kind="Internal").ap()
    kT_dram = nc.dram_tensor("k_parts_T", (3, D, KEYS), BF16, kind="Internal").ap()
    v_dram = nc.dram_tensor("v_rows", (KEYS, D), F32, kind="Internal").ap()
    with ExitStack() as ctx:
        def sb(name, shape, dt=F32):
            return ctx.enter_context(nc.sbuf_tensor(name, shape, dt))

        sq, svr, rv = sb("q_scales", [P, H, RT]), sb("v_scales", [P, D]), sb("v_scale_inverses", [P, D])
        ident, identb = sb("ident", [P, P]), sb("identb", [P, P], BF16)
        with ExitStack() as for_keys:
            of_keys, context = key_inputs(nc, for_keys, a), context_inputs(nc, for_keys, a)
            with ExitStack() as for_queries:
                of_queries = query_inputs(nc, for_queries, a)
                aoT = for_queries.enter_context(nc.sbuf_tensor("aoT", [SK, ROWS], F32))
                sparse_attention(nc, a, aoT, ident, identb, (of_queries, of_keys, *context))
                project_queries(nc, a, of_queries, aoT, sq, ident, identb, x1_dram, qT_dram)
            project_keys(nc, a, of_keys, context, svr, rv, identb, kT_dram, v_dram)
        xo = sb("xo", [P, RT, D])
        of_projection = projection_inputs(nc, ctx, a)
        cross_attention(nc, sq, svr, rv, xo, identb, of_projection, qT_dram, kT_dram, v_dram)
        y = sb("y", [P, RT, D])
        t1, t2, t3 = (sb(n, [P, 2, DC * FFN], BF16) for n in ("t1", "t2", "t3"))
        xh = sb("xh", [P, DC, ROWS], FP16)
        xl = of_projection[0][3][:].bitcast(FP16)[:, 0:DC * ROWS].rearrange("p (c n) -> p c n", c=DC)
        output_projection(nc, a, of_projection, ident, xo, y, t1, t2, t3, xh, xl, x1_dram)
        feed_forward(nc, of_projection[0][2], y, t1, t2, t3, xh, xl, out)


def kernel(**inputs):
    import numpy as _np
    import ml_dtypes as _ml
    import concourse.bacc as _bacc
    from concourse.bass_utils import run_bass_kernel_spmd as _run

    bf = _ml.bfloat16

    def lay(x):
        return _np.ascontiguousarray(x)

    i = {k: _np.asarray(v) for k, v in inputs.items()}
    at = _np.arange(S)
    arrays = {
        "x": lay(i["x"]), "ctxT": lay(i["ctx_2048"].reshape(KEYS, D).T),
        "W1T": lay(i["L0_attn_W1"].T), "WqkvT": lay(i["L0_attn_Wqkv"].T), "W2T": lay(i["L0_attn_W2"].T),
        "W3": lay(i["L0_attn_W3"]), "WoutT": lay(i["L0_attn_Wout"].T),
        "gamma": lay(i["L0_attn_gamma"].reshape(DC, P).T), "beta": lay(i["L0_attn_beta"].reshape(DC, P).T),
        "b1": lay(i["L0_attn_b1"]), "b2": lay(i["L0_attn_b2"]), "b3": lay(i["L0_attn_b3"]),
        "bqkv": lay(i["L0_attn_bqkv"]), "bout": lay(i["L0_attn_bout"]),
        "Wq": lay(i["L0_xattn_Wq"]), "bq": lay(i["L0_xattn_bq"]), "Wkv": lay(i["L0_xattn_Wkv"]),
        "bkv": lay(i["L0_xattn_bkv"]), "Wp": lay(i["L0_xattn_Wp"]), "bp": lay(i["L0_xattn_bp"]),
        "w1T": lay(i["L0_ffn_w1"].T), "w2T": lay(i["L0_ffn_w2"].T), "w3T": lay(i["L0_ffn_w3"].T),
        "ident": _np.eye(P, dtype=_np.float32), "identb": _np.eye(P).astype(bf),
        "tri": (at[:, None] <= at[None]).astype(bf), "offdiag": (1 - _np.eye(S)).astype(_np.float32),
        "rank": lay(_np.broadcast_to(_np.arange(1, TOP + 1)[None, :, None], (S, TOP, S)).astype(bf)),
    }
    nc = _bacc.Bacc("TRN2", target_bir_lowering=False, num_devices=1)
    a = {k: nc.dram_tensor("in_" + k, v.shape, mybir.dt.from_np(v.dtype), kind="ExternalInput").ap()
         for k, v in arrays.items()}
    out = nc.dram_tensor("out_rows", (ROWS, D), F32, kind="ExternalOutput").ap()
    decoder(nc, a, out)
    r = _run(nc, [{"in_" + k: v for k, v in arrays.items()}], core_ids=[0])
    return r.results[0]["out_rows"].reshape(B, S, D)
```
